# Optimizing a Trainium2 kernel written in Bass

```python
import numpy as np
import jax
import jax.numpy as jnp

def _softmax(x, axis=-1):
    return jax.nn.softmax(x, axis=axis)

def _gelu(x):
    return jax.nn.gelu(x, approximate=True)

def _silu(x):
    return jax.nn.silu(x)

def _sigmoid(x):
    return jax.nn.sigmoid(x)

def _layernorm(x, axis=-1, eps=1e-05):
    m = jnp.mean(x, axis=axis, keepdims=True)
    v = jnp.var(x, axis=axis, keepdims=True)
    return (x - m) / jnp.sqrt(v + eps)

def _scatter_add(tgt, idx, src, axis=0):
    return tgt.at[idx].add(src)

def _segment_sum(src, seg, n):
    return jax.ops.segment_sum(src, seg, n)
kernel_name = 'mk_gnn_ffn_d1_gnn_r8_2a756a'

def setup_inputs(seed: int=0):
    np.random.seed(seed)
    _w = jnp.asarray

    def _rec_inputs():
        import jax
        import jax.numpy as jnp
        _gk = jax.random.key(seed)
        x = -0.0003713 + 1 * jax.random.normal(jax.random.fold_in(_gk, 1), (6250, 256), jnp.float32)
        _s = jax.random.randint(jax.random.fold_in(_gk, 2), (100000,), 0, 6250, jnp.int32)
        _d = jax.random.randint(jax.random.fold_in(_gk, 3), (100000,), 0, 6250, jnp.int32)
        _loop = jnp.arange(6250, dtype=jnp.int32)
        src = jnp.concatenate([_s, _d, _loop])
        dst = jnp.concatenate([_d, _s, _loop])
        _o = jnp.argsort(dst, stable=True)
        src = src[_o]
        dst = dst[_o]
        return (x, src, dst)
    x, src, dst = _rec_inputs()

    def _L0_gnn_setup():
        import jax, jax.numpy as jnp
        import numpy as np
        from jax.ops import segment_sum, segment_max
        N_NODES = 6250
        N_EDGES = 100000
        IN_DIM = 256
        OUT_DIM = 64
        N_HEADS = 4
        key = jax.random.key(seed)
        k1, k2, k3, k4, k5, k6 = jax.random.split(key, 6)
        h = jax.random.normal(k1, (N_NODES, IN_DIM), dtype=jnp.float32)
        src = jax.random.randint(k2, (N_EDGES,), 0, N_NODES, dtype=jnp.int32)
        dst = jax.random.randint(k3, (N_EDGES,), 0, N_NODES, dtype=jnp.int32)
        W = jax.random.normal(k4, (N_HEADS, IN_DIM, OUT_DIM), dtype=jnp.float32) * 0.05
        a_src = jax.random.normal(k5, (N_HEADS, OUT_DIM), dtype=jnp.float32) * 0.05
        a_dst = jax.random.normal(k6, (N_HEADS, OUT_DIM), dtype=jnp.float32) * 0.05
        return {'h': h, 'src': src, 'dst': dst, 'W': W, 'a_src': a_src, 'a_dst': a_dst}
    _L0_gnn_all = _L0_gnn_setup()
    _L0_gnn_in = {k: v for k, v in _L0_gnn_all.items() if k in ('W', 'a_src', 'a_dst')}
    del _L0_gnn_all

    def _L0_ffn_setup():
        import jax, jax.numpy as jnp
        import numpy as np
        B, N, D = (16, 512, 256)
        NUM_EXPERTS, TOP_K, HEADS = (4, 2, 4)
        N_EDGES = 131072
        LN_EPS = 1e-05

        def _layernorm(x, g, b):
            mu = x.mean(-1, keepdims=True)
            var = ((x - mu) ** 2).mean(-1, keepdims=True)
            return (x - mu) * jax.lax.rsqrt(var + LN_EPS) * g + b

        def _forward(x, edge_index, W_gat, att_src, att_dst, b_gat, ln_gamma, ln_beta, W1, b1, W2, b2):
            Bc, Nc, Dc = x.shape
            M = Bc * Nc
            x_flat = x.reshape(M, Dc)
            h = (x_flat @ W_gat).reshape(M, HEADS, NUM_EXPERTS)
            loops = jnp.arange(M, dtype=edge_index.dtype)
            src = jnp.concatenate([edge_index[0], loops])
            dst = jnp.concatenate([edge_index[1], loops])
            a_src = (h * att_src).sum(-1)
            a_dst = (h * att_dst).sum(-1)
            e = jax.nn.leaky_relu(a_src[src] + a_dst[dst], negative_slope=0.2)
            e_max = jax.ops.segment_max(e, dst, num_segments=M)
            ee = jnp.exp(e - e_max[dst])
            denom = jax.ops.segment_sum(ee, dst, num_segments=M)
            alpha = ee / (denom[dst] + 1e-16)
            msg = h[src] * alpha[:, :, None]
            agg = jax.ops.segment_sum(msg, dst, num_segments=M).reshape(M, HEADS * NUM_EXPERTS) + b_gat
            scores = _layernorm(agg, ln_gamma, ln_beta).reshape(M, HEADS, NUM_EXPERTS).mean(1)
            scores = scores.reshape(Bc, Nc, NUM_EXPERTS)
            topk_s, topk_i = jax.lax.top_k(scores, TOP_K)
            w = jax.nn.softmax(topk_s, axis=-1)
            out = jnp.zeros_like(x)
            for ei in range(NUM_EXPERTS):
                g = jnp.where(topk_i == ei, w, 0.0).sum(-1)
                hh = jax.nn.gelu(x @ W1[ei] + b1[ei], approximate=False)
                out = out + g[..., None] * (hh @ W2[ei] + b2[ei])
            return out
        key = jax.random.key(seed)
        ks = jax.random.split(key, 8)
        s = 0.05
        return {'x': jax.random.normal(ks[0], (B, N, D), jnp.float32), 'W_gat': jax.random.normal(ks[1], (D, HEADS * NUM_EXPERTS), jnp.float32) * s, 'att_src': jax.random.normal(ks[2], (HEADS, NUM_EXPERTS), jnp.float32) * s, 'att_dst': jax.random.normal(ks[3], (HEADS, NUM_EXPERTS), jnp.float32) * s, 'b_gat': jnp.zeros((HEADS * NUM_EXPERTS,), jnp.float32), 'ln_gamma': jnp.ones((HEADS * NUM_EXPERTS,), jnp.float32), 'ln_beta': jnp.zeros((HEADS * NUM_EXPERTS,), jnp.float32), 'W1': jax.random.normal(ks[4], (NUM_EXPERTS, D, 2 * D), jnp.float32) * s, 'b1': jnp.zeros((NUM_EXPERTS, 2 * D), jnp.float32), 'W2': jax.random.normal(ks[5], (NUM_EXPERTS, 2 * D, D), jnp.float32) * s, 'b2': jnp.zeros((NUM_EXPERTS, D), jnp.float32), 'edge_index': jax.random.randint(ks[6], (2, N_EDGES), 0, B * N, jnp.int32)}
    _L0_ffn_all = _L0_ffn_setup()
    _L0_ffn_in = {k: v for k, v in _L0_ffn_all.items() if k in ('W_gat', 'att_src', 'att_dst', 'b_gat', 'ln_gamma', 'ln_beta', 'W1', 'b1', 'W2', 'b2', 'edge_index')}
    del _L0_ffn_all
    return {'x': x, 'src': src, 'dst': dst, 'L0_gnn_W': _L0_gnn_in['W'], 'L0_gnn_a_src': _L0_gnn_in['a_src'], 'L0_gnn_a_dst': _L0_gnn_in['a_dst'], 'L0_ffn_W_gat': _L0_ffn_in['W_gat'], 'L0_ffn_att_src': _L0_ffn_in['att_src'], 'L0_ffn_att_dst': _L0_ffn_in['att_dst'], 'L0_ffn_b_gat': _L0_ffn_in['b_gat'], 'L0_ffn_ln_gamma': _L0_ffn_in['ln_gamma'], 'L0_ffn_ln_beta': _L0_ffn_in['ln_beta'], 'L0_ffn_W1': _L0_ffn_in['W1'], 'L0_ffn_b1': _L0_ffn_in['b1'], 'L0_ffn_W2': _L0_ffn_in['W2'], 'L0_ffn_b2': _L0_ffn_in['b2'], 'L0_ffn_edge_index': _L0_ffn_in['edge_index']}

def reference(x, src, dst, L0_gnn_W, L0_gnn_a_src, L0_gnn_a_dst, L0_ffn_W_gat, L0_ffn_att_src, L0_ffn_att_dst, L0_ffn_b_gat, L0_ffn_ln_gamma, L0_ffn_ln_beta, L0_ffn_W1, L0_ffn_b1, L0_ffn_W2, L0_ffn_b2, L0_ffn_edge_index):
    import jax
    import jax.numpy as jnp

    def _L0_gnn_ref(h, src, dst, W, a_src, a_dst):
        import jax, jax.numpy as jnp
        import numpy as np
        from jax.ops import segment_sum, segment_max
        N_NODES = 6250
        N_EDGES = 100000
        IN_DIM = 256
        OUT_DIM = 64
        N_HEADS = 4
        n = h.shape[0]
        z = jnp.einsum('ni,hio->nho', h, W)
        e_src = jnp.einsum('nho,ho->nh', z, a_src)
        e_dst = jnp.einsum('nho,ho->nh', z, a_dst)
        e = jax.nn.leaky_relu(e_src[src] + e_dst[dst], negative_slope=0.01)
        m = segment_max(e, dst, num_segments=n)
        e_exp = jnp.exp(e - m[dst])
        denom = segment_sum(e_exp, dst, num_segments=n)
        alpha = e_exp / denom[dst]
        msg = alpha[:, :, None] * z[src]
        out = segment_sum(msg, dst, num_segments=n)
        return out.reshape(n, N_HEADS * OUT_DIM)

    def _L0_ffn_ref(x, W_gat, att_src, att_dst, b_gat, ln_gamma, ln_beta, W1, b1, W2, b2, edge_index):
        import jax, jax.numpy as jnp
        import numpy as np
        B, N, D = (16, 512, 256)
        NUM_EXPERTS, TOP_K, HEADS = (4, 2, 4)
        N_EDGES = 131072
        LN_EPS = 1e-05

        def _layernorm(x, g, b):
            mu = x.mean(-1, keepdims=True)
            var = ((x - mu) ** 2).mean(-1, keepdims=True)
            return (x - mu) * jax.lax.rsqrt(var + LN_EPS) * g + b

        def _forward(x, edge_index, W_gat, att_src, att_dst, b_gat, ln_gamma, ln_beta, W1, b1, W2, b2):
            Bc, Nc, Dc = x.shape
            M = Bc * Nc
            x_flat = x.reshape(M, Dc)
            h = (x_flat @ W_gat).reshape(M, HEADS, NUM_EXPERTS)
            loops = jnp.arange(M, dtype=edge_index.dtype)
            src = jnp.concatenate([edge_index[0], loops])
            dst = jnp.concatenate([edge_index[1], loops])
            a_src = (h * att_src).sum(-1)
            a_dst = (h * att_dst).sum(-1)
            e = jax.nn.leaky_relu(a_src[src] + a_dst[dst], negative_slope=0.2)
            e_max = jax.ops.segment_max(e, dst, num_segments=M)
            ee = jnp.exp(e - e_max[dst])
            denom = jax.ops.segment_sum(ee, dst, num_segments=M)
            alpha = ee / (denom[dst] + 1e-16)
            msg = h[src] * alpha[:, :, None]
            agg = jax.ops.segment_sum(msg, dst, num_segments=M).reshape(M, HEADS * NUM_EXPERTS) + b_gat
            scores = _layernorm(agg, ln_gamma, ln_beta).reshape(M, HEADS, NUM_EXPERTS).mean(1)
            scores = scores.reshape(Bc, Nc, NUM_EXPERTS)
            topk_s, topk_i = jax.lax.top_k(scores, TOP_K)
            w = jax.nn.softmax(topk_s, axis=-1)
            out = jnp.zeros_like(x)
            for ei in range(NUM_EXPERTS):
                g = jnp.where(topk_i == ei, w, 0.0).sum(-1)
                hh = jax.nn.gelu(x @ W1[ei] + b1[ei], approximate=False)
                out = out + g[..., None] * (hh @ W2[ei] + b2[ei])
            return out
        return _forward(x, edge_index, W_gat, att_src, att_dst, b_gat, ln_gamma, ln_beta, W1, b1, W2, b2)
    x = x + _L0_gnn_ref(_layernorm(x, axis=-1), src, dst, L0_gnn_W, L0_gnn_a_src, L0_gnn_a_dst)
    x = x + _L0_ffn_ref(_layernorm(x, axis=-1)[None], L0_ffn_W_gat, L0_ffn_att_src, L0_ffn_att_dst, L0_ffn_b_gat, L0_ffn_ln_gamma, L0_ffn_ln_beta, L0_ffn_W1, L0_ffn_b1, L0_ffn_W2, L0_ffn_b2, L0_ffn_edge_index)[0]
    return x

_drawn_inputs = setup_inputs


def setup_inputs(seed=0):
    import zlib

    import numpy as np

    out = dict(_drawn_inputs(seed))
    spreads = {'L0_ffn_b_gat': (0.0, 0.1),
     'L0_ffn_ln_gamma': (1.0, 0.2),
     'L0_ffn_ln_beta': (0.0, 0.1),
     'L0_ffn_b1': (0.0, 0.1),
     'L0_ffn_b2': (0.0, 0.1)}
    factors = {}
    for name, (base, spread) in spreads.items():
        noise = np.random.default_rng([zlib.crc32(name.encode()), seed]).standard_normal(out[name].shape)
        drawn = base * np.exp(spread * noise) if base else spread * noise
        out[name] = jnp.asarray(drawn.astype(out[name].dtype))
    for name, factor in factors.items():
        out[name] = (out[name] * factor).astype(out[name].dtype)
    return out
```

```python
import numpy as np
import concourse.bass as bass
from concourse import mybir
from contextlib import ExitStack

F32 = mybir.dt.float32
BF16 = mybir.dt.bfloat16
I32 = mybir.dt.int32
ALU = mybir.AluOpType
ACT = mybir.ActivationFunctionType
AXX = mybir.AxisListType.X

P = 128
N_NODES = 6250
D = 256
BLOCKS = -(-N_NODES // P)
NPAD = BLOCKS * P
TAIL = N_NODES - (BLOCKS - 1) * P
TRASH = NPAD - 1
HEADS = 4
OUT_A = 64
OUT_B = 4
EXPERTS = 4
HID = 512
U = 4
GROUP = U * P
NEG = -1.0e30
LN_EPS = 1e-5
RING = 4


class Graph:

    def __init__(self, name, edges, out, slope):
        self.name = name
        self.edges = edges
        self.cols = -(-edges // P)
        self.out = out
        self.row = HEADS * (out + 1)
        self.slope = slope
        groups = -(-self.cols * P // GROUP) + BLOCKS
        self.groups = -(-groups // RING) * RING
        self.tiles = self.groups * U


class Chain:

    def __init__(self, eng, sem):
        self.eng, self.sem, self.n, self.i, self.per = eng, sem, 0, None, 0

    def loop(self, i, per):
        self.i, self.per, self.start = i, per, self.n

    def end(self, trips):
        assert self.n - self.start == self.per, (self.n - self.start, self.per)
        self.n = self.start + self.per * trips
        self.i = None

    def mark(self, ins):
        ins.then_inc(self.sem, 1)
        self.n += 1

    def __call__(self, ins):
        self.mark(ins)
        self.wait()

    def wait(self):
        self.eng.wait_ge(self.sem, self.n if self.i is None else self.i * self.per + self.n)


def build(nc, x, src, dst, gnn_W, gnn_a_src, gnn_a_dst, W_gat, att_src, att_dst, b_gat,
          ln_gamma, ln_beta, W1, b1, W2, b2, edge_index, out):
    A = Graph("a", src.shape[0], OUT_A, 0.01)
    B = Graph("b", edge_index.shape[1], OUT_B, 0.2)

    def dram(name, shape, dt):
        return nc.dram_tensor(name, shape, dt, kind="Internal").ap()

    for g in (A, B):
        g.table = dram(f"table_{g.name}", (NPAD, g.row), F32)
        g.slots = dram(f"slots_{g.name}", (P * g.tiles, 2), I32)

    ctx = ExitStack()
    with ctx:
        def sb(name, shape, dt=F32, at=ctx):
            return at.enter_context(nc.sbuf_tensor(name, shape, dt))

        def sem(name):
            return ctx.enter_context(nc.semaphore(name))

        X = sb("X", [P, BLOCKS, D])
        ACC = sb("ACC", [P, BLOCKS, A.row])
        ident = sb("ident", [P, P])
        ident_neg = sb("ident_neg", [P, P], BF16)
        iota_row = sb("iota_row", [P, P])
        accB = sb("accB", [P, BLOCKS, B.row])
        for g in (A, B):
            g.ed = sb(f"ed_{g.name}", [P, BLOCKS, HEADS])
            g.mx = sb(f"mx_{g.name}", [P, BLOCKS, HEADS])
            g.blk = sb(f"blk_{g.name}", [P, g.groups], I32)
        A.acc, B.acc = ACC, accB

        index_and_nodes(nc, ctx, sb, sem, A, B, X, ident, ident_neg, iota_row,
                        x, src, dst, edge_index, gnn_W, gnn_a_src, gnn_a_dst)
        attend(nc, sem, A, ident, ident_neg, iota_row)
        nodes_b(nc, sem, A, B, X, ident, W_gat, att_src, att_dst)
        attend(nc, sem, B, ident, ident_neg, iota_row)
        experts(nc, sem, A, B, X, b_gat, ln_gamma, ln_beta, W1, b1, W2, b2, out)


def index_and_nodes(nc, ctx, sb, sem, A, B, X, ident, ident_neg, iota_row,
                    x, src, dst, edge_index, gnn_W, gnn_a_src, gnn_a_dst):
    ph = ExitStack()
    with ph:
        def tb(name, shape, dt=F32):
            return sb(name, shape, dt, ph)

        SC = 4
        T = A.cols
        flat = A.acc[:, :, :].rearrange("p b f -> p (b f)")
        dst_i = flat[:, 0:T].bitcast(I32)
        hi = flat[:, T:2 * T]
        mask = flat[:, 2 * T:3 * T]
        scan = flat[:, 3 * T:4 * T]
        pos = flat[:, 4 * T:5 * T]
        part = flat[:, 5 * T:6 * T]
        ones_t = flat[:, 6 * T:7 * T]
        for g in (A, B):
            g.rec = tb(f"rec_{g.name}", [P, g.cols, 3], I32)
            g.rowtot = tb(f"rowtot_{g.name}", [P, BLOCKS])
            g.start = tb(f"start_{g.name}", [P, BLOCKS])
            g.gend = tb(f"gend_{g.name}", [P, BLOCKS])
        maxg = max(A.groups, B.groups)
        iota_g = tb("iota_g", [P, maxg])
        blkf = tb("blkf", [P, maxg])
        bcol = tb("bcol", [P, BLOCKS])
        ones_mat = tb("ones_mat", [P, P])
        lower = tb("lower", [P, P])
        small = tb("small", [P, 4, BLOCKS])
        small_i = tb("small_i", [P, BLOCKS], I32)
        fill = tb("fill", [P, 512, 2], I32)
        stage = tb("stage", [P, 2, SC, 3], I32)
        wx = tb("wx_a", [P, 2, D + 8])
        a_bc = tb("a_bc", [P, 2, D])
        wprod = tb("wprod", [P, 2, D])
        stats = tb("stats", [P, 6])
        mv = tb("mv", [P, 2])
        sd = tb("sd", [P, 2])
        xn = tb("xn", [P, D])
        xt = tb("xt", [P, 2, P])
        ps_cnt = ph.enter_context(nc.psum_tensor("ps_cnt", [P, 512], F32))
        ps_t = ph.enter_context(nc.psum_tensor("ps_t", [P, 2, P], F32))
        ps_z = ph.enter_context(nc.psum_tensor("ps_z", [P, 512], F32))

        s_const = sem("i_const")
        s_idx = sem("i_edges_loaded")
        s_idxb = sem("i_edges_b_loaded")
        s_x = sem("i_x_loaded")
        s_w = sem("i_w_loaded")
        s_fill = sem("i_slots_filled")
        s_fillm = sem("i_fill_made")
        s_tot = sem("i_row_totals")
        s_pre = sem("i_prefixes")
        s_rec = sem("i_records")
        s_st = [sem(f"i_staged_{g.name}") for g in (A, B)]
        s_sc = [[sem(f"i_scattered_{g.name}{h}") for h in range(2)] for g in (A, B)]
        s_see = sem("i_pool_saw")
        s_dve = sem("i_dve_chain")
        s_zero = sem("i_cleared")
        s_var = sem("i_var")
        s_sd = sem("i_sd")
        s_xn = sem("i_xn")
        s_xtp = sem("i_xt_psum")
        s_xt = sem("i_xt")
        s_z = sem("i_z")
        s_zc = sem("i_z_copied")
        s_seea = sem("i_act_saw")
        s_seev = sem("i_dve_saw")
        s_tab = sem("i_table_stored")
        s_free = sem("i_scratch_free")

        fills = sum(-(-g.tiles // 512) for g in (A, B))
        ends = [[16 * SC * (-(-(g.cols // SC - h) // 2)) for h in range(2)] for g in (A, B)]

        with nc.Block() as block:
            @block.gpsimd
            def _(pool):
                nc.gpsimd.memset(fill[:, :, 0:1], 0).then_inc(s_fillm, 1)
                nc.gpsimd.memset(fill[:, :, 1:2], -1).then_inc(s_fillm, 1)
                nc.gpsimd.memset(ident[:], 0.0).then_inc(s_const, 1)
                nc.gpsimd.memset(lower[:], 1.0).then_inc(s_const, 1)
                nc.gpsimd.memset(ones_mat[:], 1.0).then_inc(s_const, 1)
                pool.wait_ge(s_const, 3)
                nc.gpsimd.affine_select(out=ident[:], in_=ident[:], compare_op=ALU.not_equal, fill=1.0,
                                        base=0, pattern=[[-1, P]], channel_multiplier=1).then_inc(s_const, 1)
                nc.gpsimd.affine_select(out=lower[:], in_=lower[:], compare_op=ALU.is_gt, fill=0.0,
                                        base=0, pattern=[[1, P]], channel_multiplier=-1).then_inc(s_const, 1)
                nc.gpsimd.iota(iota_row[:], pattern=[[1, P]], base=0, channel_multiplier=0,
                               allow_small_or_imprecise_dtypes=True).then_inc(s_const, 1)
                nc.gpsimd.iota(bcol[:], pattern=[[1, BLOCKS]], base=0, channel_multiplier=0,
                               allow_small_or_imprecise_dtypes=True).then_inc(s_const, 1)
                nc.gpsimd.iota(iota_g[:], pattern=[[1, maxg]], base=0, channel_multiplier=0,
                               allow_small_or_imprecise_dtypes=True).then_inc(s_const, 1)
                pool.wait_ge(s_const, 8)
                pool.wait_ge(s_fill, 16 * fills)
                for n, g in enumerate((A, B)):
                    pool.wait_ge(s_rec, n + 1)
                    turns = g.cols // (2 * SC)

                    def scatter(i, h):
                        at = i * (2 * SC) + h * SC
                        cols = slice(at, at + SC) if isinstance(i, int) else bass.ds(at, SC)
                        nc.gpsimd.tensor_copy(stage[:, h], g.rec[:, cols, :]).then_inc(s_st[n], 1)
                        pool.wait_ge(s_st[n], i * 2 + (h + 1))
                        pool.sem_inc(s_see, 1)
                        for c in range(SC):
                            pool.indirect_dma_start(
                                out=g.slots[:, :],
                                out_offset=bass.IndirectOffsetOnAxis(ap=stage[:, h, c, 0:1], axis=0),
                                in_=stage[:, h, c, 1:3], in_offset=None).then_inc(s_sc[n][h], 16)

                    for h in range(2):
                        if n:
                            pool.wait_ge(s_sc[0][h], ends[0][h])
                        scatter(0, h)
                    with pool.Fori(1, turns) as i:
                        for h in range(2):
                            pool.wait_ge(s_sc[n][h], i * (16 * SC))
                            pool.sem_inc(s_see, 1)
                            scatter(i, h)
                    if g.cols > turns * 2 * SC:
                        assert g.cols == turns * 2 * SC + SC
                        pool.wait_ge(s_sc[n][0], turns * 16 * SC)
                        scatter(turns, 0)
                for n in range(2):
                    for h in range(2):
                        pool.wait_ge(s_sc[n][h], ends[n][h])


            @block.sync
            def _(sp):
                sp.wait_ge(s_zero, 1)
                full = A.edges // A.cols
                sp.dma_start(dst_i[0:full, :], dst[0:full * A.cols].rearrange("(p t) -> p t", t=A.cols)).then_inc(s_idx, 16)
                sp.dma_start(pos[0:full, :].bitcast(I32), src[0:full * A.cols].rearrange("(p t) -> p t", t=A.cols)).then_inc(s_idx, 16)
                rest = A.edges - full * A.cols
                assert full < P
                sp.dma_start(dst_i[full:full + 1, 0:rest], dst[full * A.cols:A.edges].rearrange("(p t) -> p t", p=1)).then_inc(s_idx, 16)
                sp.dma_start(pos[full:full + 1, 0:rest].bitcast(I32), src[full * A.cols:A.edges].rearrange("(p t) -> p t", p=1)).then_inc(s_idx, 16)
                sp.dma_start(X[:, 0:BLOCKS - 1, :], x[0:(BLOCKS - 1) * P, :].rearrange("(b p) f -> p b f", p=P)).then_inc(s_x, 16)
                sp.dma_start(X[0:TAIL, BLOCKS - 1, :], x[(BLOCKS - 1) * P:N_NODES, :]).then_inc(s_x, 16)
                for k in range(2):
                    sp.dma_start(wx[:, k, 0:D].rearrange("p (h o) -> p h o", h=HEADS),
                                 gnn_W[:, k * P:(k + 1) * P, :].rearrange("h p o -> p h o")).then_inc(s_w, 16)
                for n, a in enumerate((gnn_a_src, gnn_a_dst)):
                    sp.dma_start(a_bc[:, n, :], a.rearrange("(u h) o -> u (h o)", u=1).to_broadcast([P, D])).then_inc(s_w, 16)
                sp.wait_ge(s_fillm, 2)
                for g in (A, B):
                    view = g.slots.rearrange("(p t) c -> p t c", p=P)
                    for t in range(0, g.tiles, 512):
                        w = min(512, g.tiles - t)
                        sp.dma_start(view[:, t:t + w, :], fill[:, 0:w, :]).then_inc(s_fill, 16)
                sp.wait_ge(s_rec, 1)
                for n, t in enumerate((pos, dst_i)):
                    t = t if n else t.bitcast(I32)
                    sp.dma_start(t[:, 0:B.cols], edge_index[n, :].rearrange("(p t) -> p t", t=B.cols)).then_inc(s_idxb, 16)
                sp.wait_ge(s_zc, BLOCKS)
                sp.dma_start(A.table.rearrange("(b p) f -> p b f", p=P), A.acc[:, :, :]).then_inc(s_tab, 16)
                sp.wait_ge(s_tab, 16)

            @block.vector
            def _(dve):
                link = Chain(dve, s_dve)
                nc.vector.memset(X[:, BLOCKS - 1, :], 0.0)
                nc.vector.memset(dst_i, TRASH)
                nc.vector.memset(pos.bitcast(I32), 0).then_inc(s_zero, 1)
                link(nc.vector.memset(ones_t, 1.0))
                dve.wait_ge(s_const, 8)
                nc.vector.tensor_scalar(ident_neg[:], ident[:], NEG, None, ALU.mult)
                for n, g in enumerate((A, B)):
                    T = g.cols
                    if n == 0:
                        dve.wait_ge(s_idx, 64)
                    else:
                        dve.wait_ge(s_idxb, 32)
                    nc.vector.tensor_scalar(g.rec[:, :, 1], pos[:, 0:T].bitcast(I32), N_NODES - 1, None, ALU.min)
                    link(nc.vector.tensor_scalar(dst_i[:, 0:T], dst_i[:, 0:T], TRASH, None, ALU.min))
                    link(nc.vector.tensor_scalar(g.rec[:, :, 2], dst_i[:, 0:T], P - 1, None, ALU.bitwise_and))
                    link(nc.vector.tensor_scalar(dst_i[:, 0:T], dst_i[:, 0:T], 7, None, ALU.logical_shift_right))
                    link(nc.vector.tensor_copy(hi[:, 0:T], dst_i[:, 0:T]))
                    link(nc.vector.memset(pos[:, 0:T], 0.0))
                    with dve.Fori(0, BLOCKS) as b:
                        link.loop(b, 2)
                        link(nc.vector.tensor_scalar(mask[:, 0:T], hi[:, 0:T], bcol[:, bass.ds(b, 1)], None, ALU.is_equal))
                        link(nc.vector.tensor_reduce(g.rowtot[:, bass.ds(b, 1)], mask[:, 0:T], AXX, ALU.add))
                        link.end(BLOCKS)
                    nc.vector.tensor_scalar(mask[:, 0:1], hi[:, 0:1], 0.0, None, ALU.mult).then_inc(s_tot, 1)
                    dve.wait_ge(s_pre, n + 1)
                    link(nc.vector.tensor_scalar(small_i[:], ps_cnt[:, 0:BLOCKS], float(GROUP - 1), None, ALU.add))
                    link(nc.vector.tensor_scalar(small_i[:], small_i[:], GROUP.bit_length() - 1, None, ALU.logical_shift_right))
                    link(nc.vector.tensor_copy(small[:, 0, :], small_i[:]))
                    link(nc.vector.tensor_tensor_scan(g.gend[:], ones_t[:, 0:BLOCKS], small[:, 0, :], 0.0, ALU.mult, ALU.add))
                    link(nc.vector.tensor_tensor(small[:, 1, :], g.gend[:], small[:, 0, :], ALU.subtract))
                    link(nc.vector.tensor_scalar(small[:, 2, :], small[:, 1, :], float(GROUP), -1.0, ALU.mult, ALU.add))
                    link(nc.vector.tensor_tensor(g.start[:], ps_cnt[:, 64:64 + BLOCKS], small[:, 2, :], ALU.add))
                    link(nc.vector.memset(blkf[:], 0.0))
                    with dve.Fori(0, BLOCKS) as b:
                        link.loop(b, 5)
                        link(nc.vector.tensor_scalar(mask[:, 0:T], hi[:, 0:T], bcol[:, bass.ds(b, 1)], None, ALU.is_equal))
                        link(nc.vector.tensor_tensor_scan(scan[:, 0:T], ones_t[:, 0:T], mask[:, 0:T], g.start[:, bass.ds(b, 1)], ALU.mult, ALU.add))
                        link(nc.vector.tensor_tensor(part[:, 0:T], mask[:, 0:T], scan[:, 0:T], ALU.mult))
                        link(nc.vector.tensor_tensor(pos[:, 0:T], pos[:, 0:T], part[:, 0:T], ALU.add))
                        link(nc.vector.scalar_tensor_tensor(blkf[:, 0:g.groups], iota_g[:, 0:g.groups], g.gend[:, bass.ds(b, 1)],
                                                            blkf[:, 0:g.groups], ALU.is_ge, ALU.add))
                        link.end(BLOCKS)
                    link(nc.vector.tensor_scalar(g.blk[:], blkf[:, 0:g.groups], float(BLOCKS - 1), None, ALU.min))
                    link(nc.vector.tensor_copy(dst_i[:, 0:T], pos[:, 0:T]))
                    link(nc.vector.tensor_scalar(part[:, 0:T].bitcast(I32), dst_i[:, 0:T], P - 1, None, ALU.bitwise_and))
                    link(nc.vector.tensor_scalar(dst_i[:, 0:T], dst_i[:, 0:T], 7, None, ALU.logical_shift_right))
                    link(nc.vector.tensor_scalar(mask[:, 0:T], part[:, 0:T].bitcast(I32), float(g.tiles), None, ALU.mult))
                    link(nc.vector.tensor_tensor(g.rec[:, :, 0], mask[:, 0:T], dst_i[:, 0:T], ALU.add))
                    nc.vector.memset(g.mx[:], NEG).then_inc(s_rec, 1)

                dve.wait_ge(s_w, 64)
                for k in range(2):
                    for n in range(2):
                        link(nc.vector.tensor_tensor(wprod[:, n, :], wx[:, k, 0:D], a_bc[:, n, :], ALU.mult))
                        link(nc.vector.tensor_reduce(wx[:, k, D + 4 * n:D + 4 * n + 4],
                                                     wprod[:, n, :].rearrange("p (h o) -> p h o", h=HEADS), AXX, ALU.add))
                dve.wait_ge(s_x, 32)
                with dve.Fori(0, BLOCKS) as b:
                    link.loop(b, 3)
                    dve.sem_inc(s_seev, 1)
                    link(nc.vector.bn_stats(stats[:], X[:, bass.ds(b, 1), :].rearrange("p b f -> p (b f)")))
                    dve.sem_inc(s_seev, 1)
                    link(nc.vector.bn_aggr(mv[:], stats[:]))
                    nc.vector.tensor_scalar(sd[:, 0:1], mv[:, 1:2], LN_EPS, None, ALU.add).then_inc(s_var, 1)
                    dve.wait_ge(s_sd, b + 1)
                    link(nc.vector.reciprocal(sd[:, 1:2], sd[:, 1:2]))
                    nc.vector.tensor_scalar(xn[:], X[:, bass.ds(b, 1), :].rearrange("p b f -> p (b f)"), mv[:, 0:1], sd[:, 1:2],
                                            ALU.subtract, ALU.mult).then_inc(s_xn, 1)
                    dve.wait_ge(s_z, b + 1)
                    nc.vector.tensor_scalar(A.acc[:, bass.ds(b, 1), :].rearrange("p b (h o) -> p (b h) o", h=HEADS)[:, :, 0:OUT_A],
                                            ps_z[:, 0:D].rearrange("p (h o) -> p h o", h=HEADS), 1.0, None, ALU.mult)
                    nc.vector.tensor_scalar(A.acc[:, bass.ds(b, 1), :].rearrange("p b (h o) -> p (b h) o", h=HEADS)[:, :, OUT_A],
                                            ps_z[:, D:D + 4], 1.0, None, ALU.mult)
                    nc.vector.tensor_scalar(A.ed[:, bass.ds(b, 1), :].rearrange("p b h -> p (b h)"), ps_z[:, D + 4:D + 8],
                                            1.0, None, ALU.mult).then_inc(s_zc, 1)
                    link.end(BLOCKS)

            @block.scalar
            def _(act):
                with act.Fori(0, BLOCKS) as b:
                    act.wait_ge(s_var, b + 1)
                    nc.scalar.activation(sd[:, 1:2], sd[:, 0:1], ACT.Sqrt).then_inc(s_sd, 1)
                    act.wait_ge(s_xtp, b + 1)
                    nc.scalar.activation(xt[:], ps_t[:], ACT.Copy).then_inc(s_xt, 1)

            @block.tensor
            def _(pe):
                pe.wait_ge(s_const, 8)
                for n, g in enumerate((A, B)):
                    pe.wait_ge(s_tot, n + 1)
                    nc.tensor.matmul(ps_cnt[:, 0:BLOCKS], ones_mat[:], g.rowtot[:], start=True, stop=True)
                    nc.tensor.matmul(ps_cnt[:, 64:64 + BLOCKS], lower[:], g.rowtot[:], start=True, stop=True).then_inc(s_pre, 1)
                with pe.Fori(0, BLOCKS) as b:
                    pe.wait_ge(s_xn, b + 1)
                    for k in range(2):
                        last = nc.tensor.transpose(ps_t[:, k, :], xn[:, k * P:(k + 1) * P], ident[:])
                    last.then_inc(s_xtp, 1)
                    pe.wait_ge(s_xt, b + 1)
                    for k in range(2):
                        last = nc.tensor.matmul(ps_z[:, 0:D + 8], xt[:, k, :], wx[:, k, :], start=(k == 0), stop=(k == 1))
                    last.then_inc(s_z, 1)


def attend(nc, sem, g, ident, ident_neg, iota_row):
    ph = ExitStack()
    n_ = g.name
    G = g.groups
    with ph:
        def tb(name, shape, dt=F32):
            return ph.enter_context(nc.sbuf_tensor(name + "_" + n_, shape, dt))

        def pt(name, shape):
            return ph.enter_context(nc.psum_tensor(name + "_" + n_, shape, F32))

        o1 = g.out + 1
        dve_tiles = U - 1 if g.out > 16 else U
        slots = tb("slots_sb", [P, g.tiles, 2], I32)
        dl = tb("dl", [P, g.tiles + U])
        st = tb("st", [P, RING, U], I32)
        rows = tb("rows", [P, RING, U * HEADS, o1])
        msg = tb("msg", [P, 2, U * HEADS, o1])
        onehot = tb("onehot", [P, RING, U, P])
        other = tb("other", [P, 2, U, P], BF16)
        onehot_t = tb("onehot_t", [P, 2, U, P])
        tmax4 = tb("tmax4", [P, U, HEADS])
        tmax = tb("tmax", [P, 4, HEADS])
        node = tb("node", [P, 2, 2 * HEADS])
        drop = tb("drop", [P, RING, HEADS])
        scale = tb("scale", [P, RING, HEADS])
        u = tb("u", [P, 4, U * HEADS])
        ps_es = pt("ps_es", [P, U, HEADS, P])
        ps_ot = pt("ps_ot", [P, U, P])
        ps_ge = pt("ps_ge", [P, 2, U, 2 * HEADS])
        ps_out = pt("ps_out", [P, 2, 512])

        def sm(name):
            return sem(name + "_" + n_)

        s_sl, s_dl, s_clear = sm("slots_loaded"), sm("dl_ready"), sm("acc_cleared")
        s_st, s_see = sm("indices_staged"), sm("pool_saw")
        s_rows = [sm(f"rows_gathered{q}") for q in range(RING)]
        s_oh, s_oth = sm("onehot_ready"), sm("other_ready")
        s_otp, s_ot = sm("onehot_t_psum"), sm("onehot_t_ready")
        s_es, s_mx = sm("scores_spread"), sm("scores_maxed")
        s_drop, s_node, s_scale = sm("drop_ready"), sm("node_ready"), sm("scale_ready")
        s_ge, s_u, s_ex, s_msg = sm("edge_values"), sm("exponent_ready"), sm("weight_ready"), sm("msg_ready")
        s_out, s_acc = sm("sums_ready"), sm("sums_added")
        s_msga = sm("msg_by_act_ready")
        s_dve = sm("dve_chain")
        trips = G // RING - 1

        def steps(eng, step):
            for it in range(RING):
                step(it, it, it >= 1, it >= 2, True)
            with eng.Fori(0, trips) as i:
                yield i
                for v in range(RING):
                    step(i * RING + (RING + v), v, True, True, True)
            step(G, 0, True, True, False)
            step(G + 1, 1, False, True, False)

        with nc.Block() as block:
            @block.sync
            def _(sp):
                sp.dma_start(slots[:], g.slots.rearrange("(p t) c -> p t c", p=P)).then_inc(s_sl, 16)

            @block.gpsimd
            def _(pool):
                pool.wait_ge(s_sl, 16)

                def gather(i, q):
                    nc.gpsimd.tensor_copy(st[:, q, :], slots[:, bass.ds(i * (RING * U) + q * U, U), 0]
                                          if not isinstance(i, int) else
                                          slots[:, i * RING * U + q * U:i * RING * U + (q + 1) * U, 0]).then_inc(s_st, 1)
                    pool.wait_ge(s_st, i * RING + (q + 1))
                    pool.sem_inc(s_see, 1)
                    for j in range(U):
                        pool.indirect_dma_start(
                            out=rows[:, q, j * HEADS:(j + 1) * HEADS, :].rearrange("p h o -> p (h o)"), out_offset=None,
                            in_=g.table[:, :],
                            in_offset=bass.IndirectOffsetOnAxis(ap=st[:, q, j:j + 1], axis=0)).then_inc(s_rows[q], 16)

                for q in range(RING):
                    gather(0, q)
                with pool.Fori(0, trips) as i:
                    for q in range(RING):
                        pool.wait_ge(s_msg, i * RING + (q + 1))
                        if dve_tiles < U:
                            pool.wait_ge(s_msga, i * RING + (q + 1))
                        pool.sem_inc(s_see, 1)
                        gather(i + 1, q)

            @block.vector
            def _(dve):
                link = Chain(dve, s_dve)
                dve.wait_ge(s_sl, 16)
                nc.vector.memset(dl[:, g.tiles:], -1.0)
                if g.name == "a":
                    nc.vector.memset(g.acc[:, :, :], 0.0)
                link(nc.vector.tensor_copy(dl[:, 0:g.tiles], slots[:, :, 1]))

                def make_onehot(it, q):
                    if not isinstance(it, int) or it >= RING:
                        dve.wait_ge(s_out, it - (RING - 1))
                    c = bass.ds(it * U, U) if not isinstance(it, int) else slice(it * U, it * U + U)
                    nc.vector.tensor_tensor(onehot[:, q], iota_row[:].unsqueeze(1).to_broadcast([P, U, P]),
                                            dl[:, c].unsqueeze(2).to_broadcast([P, U, P]), ALU.is_equal).then_inc(s_oh, 1)

                def block_of(grp):
                    c = bass.ds(grp, 1) if not isinstance(grp, int) else slice(grp, grp + 1)
                    return dve.value_load(g.blk[0:1, c], min_val=0, max_val=BLOCKS - 1)

                def at(t, b):
                    return t[:, bass.ds(b, 1), :].rearrange("p b f -> p (b f)")

                def step(it, q, prev, prev2, now):
                    static = isinstance(it, int)
                    p, r = (q - 1) % 2, (q - 1) % RING
                    p2, r2 = q % 2, (q - 2) % RING
                    new = node[:, q % 2, :]
                    if now:
                        make_onehot(it + 1, (q + 1) % RING)
                        b = block_of(it)
                    if prev2:
                        b2 = block_of(it - 2)
                        a = g.acc[:, bass.ds(b2, 1), :].rearrange("p b (h o) -> p (b h) o", h=HEADS)
                    if now:
                        for j in range(U):
                            dve.wait_ge(s_es, it * U + (j + 1))
                            nc.vector.tensor_reduce(tmax4[:, j, :], ps_es[:, j], AXX, ALU.max).then_inc(s_mx, 1)
                    if prev2:
                        dve.wait_ge(s_scale, it - 1)
                        if not static or it >= 3:
                            dve.wait_ge(s_acc, it - 2)
                        link.mark(nc.vector.tensor_tensor(a, a, scale[:, r2, :].unsqueeze(2).to_broadcast([P, HEADS, o1]), ALU.mult))
                    if now:
                        dve.wait_ge(s_mx, it * U + U)
                        link.mark(nc.vector.tensor_reduce(tmax[:, 0, :], tmax4[:].rearrange("p j h -> p h j"), AXX, ALU.max))
                    if prev:
                        dve.wait_ge(s_ge, it)
                        u4 = [u[:, n, :].rearrange("p (j h) -> p j h", j=U) for n in range(3)]
                        link.mark(nc.vector.tensor_tensor(u4[0], ps_ge[:, p, :, 0:HEADS],
                                                          rows[:, r, :, g.out].rearrange("p (j h) -> p j h", j=U), ALU.add))
                    link.wait()
                    if now:
                        link.mark(nc.vector.tensor_tensor(tmax[:, 1, :], tmax[:, 0, :], at(g.ed, b), ALU.add))
                    if prev:
                        link.mark(nc.vector.scalar_tensor_tensor(u[:, 1, :], u[:, 0, :], g.slope, u[:, 0, :], ALU.mult, ALU.max))
                        link.wait()
                        link.mark(nc.vector.tensor_tensor(u4[2], u4[1], ps_ge[:, p, :, HEADS:], ALU.subtract))
                    if now:
                        if not prev:
                            link.wait()
                        link.mark(nc.vector.scalar_tensor_tensor(tmax[:, 2, :], tmax[:, 1, :], g.slope, tmax[:, 1, :], ALU.mult, ALU.max))
                    link.wait()
                    if prev:
                        nc.vector.tensor_scalar(u[:, 3, :], u[:, 2, :], 0.0, None, ALU.min).then_inc(s_u, 1)
                    if now:
                        link(nc.vector.tensor_tensor(new[:, HEADS:], tmax[:, 2, :], at(g.mx, b), ALU.max))
                        nc.vector.tensor_tensor(drop[:, q, :], at(g.mx, b), new[:, HEADS:], ALU.subtract).then_inc(s_drop, 1)
                        nc.vector.tensor_scalar(new[:, 0:HEADS], at(g.ed, b), 1.0, None, ALU.mult).then_inc(s_node, 1)
                        dve.wait_ge(s_drop, it + 1)
                        link.mark(nc.vector.tensor_scalar(at(g.mx, b), new[:, HEADS:], 1.0, None, ALU.mult))
                    if prev:
                        dve.wait_ge(s_ex, it)
                        mine = slice(0, dve_tiles * HEADS)
                        nc.vector.tensor_tensor(msg[:, p, mine, 0:g.out], rows[:, r, mine, 0:g.out],
                                                msg[:, p, mine, g.out:].to_broadcast([P, dve_tiles * HEADS, g.out]),
                                                ALU.mult).then_inc(s_msg, 1)
                    link.wait()
                    if prev2:
                        dve.wait_ge(s_out, it - 1)
                        nc.vector.tensor_tensor(a, a, ps_out[:, p2, 0:g.row].rearrange("p (h o) -> p h o", h=HEADS), ALU.add).then_inc(s_acc, 1)

                make_onehot(0, 0)
                for it in range(RING):
                    step(it, it, it >= 1, it >= 2, True)
                with dve.Fori(0, trips) as i:
                    link.loop(i, RING * 9)
                    for v in range(RING):
                        step(i * RING + (RING + v), v, True, True, True)
                    link.end(trips)
                step(G, 0, True, True, False)
                step(G + 1, 1, False, True, False)

            @block.scalar
            def _(act):
                def other_of(it, q):
                    act.wait_ge(s_oh, it + 1)
                    if not isinstance(it, int) or it >= 2:
                        act.wait_ge(s_es, it * U - U)
                    nc.scalar.activation(other[:, q % 2], onehot[:, q], ACT.Identity, bias=1.0, scale=-1.0).then_inc(s_oth, 1)

                def step(it, q, prev, prev2, now):
                    static = isinstance(it, int)
                    if now:
                        other_of(it + 1, (q + 1) % RING)
                        act.wait_ge(s_otp, it + 1)
                        if not static or it >= 2:
                            act.wait_ge(s_ge, it - 1)
                        nc.scalar.activation(onehot_t[:, q % 2], ps_ot[:], ACT.Copy).then_inc(s_ot, 1)
                        act.wait_ge(s_drop, it + 1)
                        if not static or it >= RING:
                            act.wait_ge(s_acc, it - (RING - 1))
                        nc.scalar.activation(scale[:, q, :], drop[:, q, :], ACT.Exp).then_inc(s_scale, 1)
                    if prev:
                        act.wait_ge(s_u, it)
                        if not static or it >= 3:
                            act.wait_ge(s_out, it - 2)
                        p, r = (q - 1) % 2, (q - 1) % RING
                        nc.scalar.activation(msg[:, p, :, g.out], u[:, 3, :], ACT.Exp).then_inc(s_ex, 1)
                        act.wait_ge(s_ex, it)
                        for n in range(dve_tiles * HEADS, U * HEADS):
                            last = nc.scalar.activation(msg[:, p, n, 0:g.out], rows[:, r, n, 0:g.out], ACT.Copy,
                                                        scale=msg[:, p, n, g.out:])
                            if n == U * HEADS - 1:
                                last.then_inc(s_msga, 1)

                other_of(0, 0)
                for it in range(RING):
                    step(it, it, it >= 1, it >= 2, True)
                with act.Fori(0, trips) as i:
                    for v in range(RING):
                        step(i * RING + (RING + v), v, True, True, True)
                step(G, 0, True, True, False)

            @block.tensor
            def _(pe):
                def step(it, i, q, prev, prev2, now):
                    static = isinstance(it, int)
                    if now:
                        pe.wait_ge(s_oth, it + 1)
                        if not static or it >= 1:
                            pe.wait_ge(s_ot, it)
                        for j in range(U):
                            last = nc.tensor.transpose(ps_ot[:, j, :], onehot[:, q, j, :], ident[:])
                        last.then_inc(s_otp, 1)
                        pe.wait_ge(s_rows[q], (i + 1) * (16 * U))
                        for j in range(U):
                            if not static or it >= 1:
                                pe.wait_ge(s_mx, it * U + (j + 1 - U))
                            for h in range(HEADS):
                                nc.tensor.matmul(ps_es[:, j, h, :], rows[:, q, j * HEADS + h, g.out:].to_broadcast([P, P]),
                                                 ident[:], start=(h == 0), stop=False, is_transpose=True)
                            nc.tensor.matmul(ps_es[:, j], other[:, q % 2, j, :],
                                             ident_neg[:].unsqueeze(1).to_broadcast([P, HEADS, P]),
                                             start=False, stop=True).then_inc(s_es, 1)
                    if prev:
                        p = (q - 1) % 2
                        pe.wait_ge(s_ot, it)
                        pe.wait_ge(s_node, it)
                        if not static or it >= 2:
                            pe.wait_ge(s_u, it - 1)
                        for j in range(U):
                            last = nc.tensor.matmul(ps_ge[:, p, j, :], onehot_t[:, p, j, :], node[:, p, :], start=True, stop=True)
                        last.then_inc(s_ge, 1)
                    if prev2:
                        p, r = q % 2, (q - 2) % RING
                        pe.wait_ge(s_ex, it - 1)
                        pe.wait_ge(s_msg, it - 1)
                        if dve_tiles < U:
                            pe.wait_ge(s_msga, it - 1)
                        if not static or it >= 4:
                            pe.wait_ge(s_acc, it - 3)
                        for j in range(U):
                            last = nc.tensor.matmul(ps_out[:, p, 0:g.row], onehot[:, r, j, :],
                                                    msg[:, p, j * HEADS:(j + 1) * HEADS, :].rearrange("p h o -> p (h o)"),
                                                    start=(j == 0), stop=(j == U - 1))
                        last.then_inc(s_out, 1)

                for it in range(RING):
                    step(it, 0, it, it >= 1, it >= 2, True)
                with pe.Fori(0, trips) as i:
                    for v in range(RING):
                        step(i * RING + (RING + v), i + 1, v, True, True, True)
                step(G, 0, 0, True, True, False)
                step(G + 1, 0, 1, False, True, False)


def nodes_b(nc, sem, A, B, X, ident, W_gat, att_src, att_dst):
    ph = ExitStack()
    with ph:
        def tb(name, shape, dt=F32):
            return ph.enter_context(nc.sbuf_tensor("nb_" + name, shape, dt))

        K = HEADS * OUT_B
        wx = tb("wx", [P, 2, K + 8])
        a_bc = tb("a_bc", [P, 2, K])
        wprod = tb("wprod", [P, 2, K])
        rden = tb("rden", [P, 2, HEADS])
        add = tb("add", [P, D])
        stats = tb("stats", [P, 6])
        mv = tb("mv", [P, 2])
        sd = tb("sd", [P, 2])
        xn = tb("xn", [P, D])
        xt = tb("xt", [P, 2, P])
        rowsB = tb("rows", [P, BLOCKS, B.row])
        selfs = tb("self", [P, BLOCKS, HEADS])
        ps_t = ph.enter_context(nc.psum_tensor("nb_ps_t", [P, 2, P], F32))
        ps_z = ph.enter_context(nc.psum_tensor("nb_ps_z", [P, 512], F32))
        s_w = sem("nb_w_loaded")
        s_dve = sem("nb_dve_chain")
        s_seev = sem("nb_dve_saw")
        s_var, s_sd, s_xn = sem("nb_var"), sem("nb_sd"), sem("nb_xn")
        s_xtp, s_xt, s_z, s_zc = sem("nb_xt_psum"), sem("nb_xt"), sem("nb_z"), sem("nb_z_copied")
        s_tab = sem("nb_table_stored")
        with nc.Block() as block:
            @block.sync
            def _(sp):
                sp.dma_start(wx[:, :, 0:K], W_gat.rearrange("(k p) f -> p k f", p=P)).then_inc(s_w, 16)
                for n, a in enumerate((att_src, att_dst)):
                    sp.dma_start(a_bc[:, n, :], a.rearrange("(u h) o -> u (h o)", u=1).to_broadcast([P, K])).then_inc(s_w, 16)
                sp.wait_ge(s_zc, BLOCKS)
                sp.dma_start(B.table.rearrange("(b p) f -> p b f", p=P), rowsB[:]).then_inc(s_tab, 16)
                sp.wait_ge(s_tab, 16)

            @block.vector
            def _(dve):
                link = Chain(dve, s_dve)
                dve.wait_ge(s_w, 48)
                for k in range(2):
                    for n in range(2):
                        link(nc.vector.tensor_tensor(wprod[:, n, :], wx[:, k, 0:K], a_bc[:, n, :], ALU.mult))
                        link(nc.vector.tensor_reduce(wx[:, k, K + 4 * n:K + 4 * n + 4],
                                                     wprod[:, n, :].rearrange("p (h o) -> p h o", h=HEADS), AXX, ALU.add))
                with dve.Fori(0, BLOCKS) as b:
                    link.loop(b, 7)
                    xb = X[:, bass.ds(b, 1), :].rearrange("p b f -> p (b f)")
                    ab = A.acc[:, bass.ds(b, 1), :].rearrange("p b (h o) -> p (b h) o", h=HEADS)
                    link(nc.vector.tensor_scalar(rden[:, 0, :], ab[:, :, OUT_A], 1e-30, None, ALU.max))
                    link(nc.vector.reciprocal(rden[:, 1, :], rden[:, 0, :]))
                    link(nc.vector.tensor_tensor(add[:].rearrange("p (h o) -> p h o", h=HEADS), ab[:, :, 0:OUT_A],
                                                 rden[:, 1, :].unsqueeze(2).to_broadcast([P, HEADS, OUT_A]), ALU.mult))
                    link(nc.vector.tensor_tensor(xb, xb, add[:], ALU.add))
                    dve.sem_inc(s_seev, 1)
                    link(nc.vector.bn_stats(stats[:], xb))
                    dve.sem_inc(s_seev, 1)
                    link(nc.vector.bn_aggr(mv[:], stats[:]))
                    nc.vector.tensor_scalar(sd[:, 0:1], mv[:, 1:2], LN_EPS, None, ALU.add).then_inc(s_var, 1)
                    dve.wait_ge(s_sd, b + 1)
                    link(nc.vector.reciprocal(sd[:, 1:2], sd[:, 1:2]))
                    nc.vector.tensor_scalar(xn[:], xb, mv[:, 0:1], sd[:, 1:2], ALU.subtract, ALU.mult).then_inc(s_xn, 1)
                    dve.wait_ge(s_xt, b + 1)
                    nc.vector.tensor_scalar(A.acc[:, bass.ds(b, 1), 0:D].rearrange("p b f -> p (b f)"),
                                            xt[:].rearrange("p k n -> p (k n)"), 1.0, None, ALU.mult)
                    dve.wait_ge(s_z, b + 1)
                    rb = rowsB[:, bass.ds(b, 1), :].rearrange("p b (h o) -> p (b h) o", h=HEADS)
                    nc.vector.tensor_scalar(rb[:, :, 0:OUT_B], ps_z[:, 0:K].rearrange("p (h o) -> p h o", h=HEADS), 1.0, None, ALU.mult)
                    nc.vector.tensor_scalar(rb[:, :, OUT_B], ps_z[:, K:K + 4], 1.0, None, ALU.mult)
                    nc.vector.tensor_scalar(B.ed[:, bass.ds(b, 1), :].rearrange("p b h -> p (b h)"), ps_z[:, K + 4:K + 8],
                                            1.0, None, ALU.mult).then_inc(s_zc, 1)
                    link.end(BLOCKS)
                dve.wait_ge(s_zc, BLOCKS)
                rows4 = rowsB[:].rearrange("p b (h o) -> p b h o", h=HEADS)
                link(nc.vector.tensor_copy(B.acc[:, :, :], rowsB[:]))
                nc.vector.memset(B.acc[:, :, :].rearrange("p b (h o) -> p b h o", h=HEADS)[:, :, :, OUT_B], 1.0)
                link(nc.vector.tensor_tensor(selfs[:], rows4[:, :, :, OUT_B], B.ed[:, :, :], ALU.add))
                nc.vector.scalar_tensor_tensor(B.mx[:, :, :], selfs[:], B.slope, selfs[:], ALU.mult, ALU.max)

            @block.scalar
            def _(act):
                with act.Fori(0, BLOCKS) as b:
                    act.wait_ge(s_var, b + 1)
                    nc.scalar.activation(sd[:, 1:2], sd[:, 0:1], ACT.Sqrt).then_inc(s_sd, 1)
                    act.wait_ge(s_xtp, b + 1)
                    nc.scalar.activation(xt[:], ps_t[:], ACT.Copy).then_inc(s_xt, 1)

            @block.tensor
            def _(pe):
                with pe.Fori(0, BLOCKS) as b:
                    pe.wait_ge(s_xn, b + 1)
                    for k in range(2):
                        last = nc.tensor.transpose(ps_t[:, k, :], xn[:, k * P:(k + 1) * P], ident[:])
                    last.then_inc(s_xtp, 1)
                    pe.wait_ge(s_xt, b + 1)
                    for k in range(2):
                        last = nc.tensor.matmul(ps_z[:, 0:K + 8], xt[:, k, :], wx[:, k, :], start=(k == 0), stop=(k == 1))
                    last.then_inc(s_z, 1)


def experts(nc, sem, A, B, X, b_gat, ln_gamma, ln_beta, W1, b1, W2, b2, out):
    ph = ExitStack()
    with ph:
        def tb(name, shape, dt=F32):
            return ph.enter_context(nc.sbuf_tensor("ex_" + name, shape, dt))

        K = HEADS * OUT_B
        FC = HID // P
        w1 = tb("w1", [P, EXPERTS, 2, HID])
        w2 = tb("w2", [P, EXPERTS, FC, D])
        b1c = tb("b1c", [P, EXPERTS, FC])
        b2b = tb("b2b", [P, EXPERTS, D])
        vec = tb("vec", [P, 3, K])
        w_ = [tb(f"wk{i}", [P, BLOCKS, K]) for i in range(2)]
        c_ = [tb(f"ck{i}", [P, BLOCKS]) for i in range(6)]
        rden = tb("rden", [P, BLOCKS, HEADS])
        sc = tb("sc", [P, EXPERTS, BLOCKS])
        rank = tb("rank", [P, EXPERTS, BLOCKS])
        gate = tb("gate", [P, BLOCKS, EXPERTS])
        hid = tb("hid", [P, 2, FC, P])
        y = tb("y", [P, 2, D])
        ps_h = ph.enter_context(nc.psum_tensor("ex_ps_h", [P, 2, FC, P], F32))
        ps_y = ph.enter_context(nc.psum_tensor("ex_ps_y", [P, 2, 512], F32))
        s_w, s_w1, s_v = sem("ex_w_loaded"), sem("ex_w1_loaded"), sem("ex_vectors_loaded")
        s_dve, s_va, s_sa, s_sub, s_exp = sem("ex_dve_chain"), sem("ex_var"), sem("ex_std"), sem("ex_sub"), sem("ex_exp")
        s_hp, s_h, s_y, s_add, s_o = sem("ex_hidden_psum"), sem("ex_hidden"), sem("ex_y"), sem("ex_added"), sem("ex_stored")
        with nc.Block() as block:
            @block.sync
            def _(sp):
                for e in range(EXPERTS):
                    sp.dma_start(w1[:, e], W1[e].rearrange("(k p) f -> p k f", p=P)).then_inc(s_w1, 16)
                for e in range(EXPERTS):
                    sp.dma_start(b1c[:, e, :], b1[e:e + 1, :].rearrange("u (c p) -> p (u c)", p=P), allow_slow_non_contiguous=True).then_inc(s_w, 16)
                    sp.dma_start(w2[:, e], W2[e].rearrange("(c p) f -> p c f", p=P)).then_inc(s_w, 16)
                sp.dma_start(b2b[:].rearrange("p e f -> p (e f)"), b2.rearrange("(u e) f -> u (e f)", u=1).to_broadcast([P, EXPERTS * D])).then_inc(s_w, 16)
                for n, v in enumerate((b_gat, ln_gamma, ln_beta)):
                    sp.dma_start(vec[:, n, :], v.rearrange("(u f) -> u f", u=1).to_broadcast([P, K])).then_inc(s_v, 16)
                sp.wait_ge(s_add, BLOCKS * EXPERTS)
                sp.dma_start(out[0:(BLOCKS - 1) * P, :].rearrange("(b p) f -> p b f", p=P), X[:, 0:BLOCKS - 1, :]).then_inc(s_o, 16)
                sp.dma_start(out[(BLOCKS - 1) * P:N_NODES, :], X[0:TAIL, BLOCKS - 1, :]).then_inc(s_o, 16)
                sp.wait_ge(s_o, 32)

            @block.vector
            def _(dve):
                link = Chain(dve, s_dve)
                V = nc.vector
                dve.wait_ge(s_v, 48)
                acc4 = B.acc[:, :, :].rearrange("p b (h o) -> p b h o", h=HEADS)
                link(V.tensor_scalar(rden[:], acc4[:, :, :, OUT_B], 1e-16, None, ALU.add))
                link(V.reciprocal(rden[:], rden[:]))
                agg = w_[0][:]
                for h in range(HEADS):
                    V.tensor_tensor(agg[:, :, h * OUT_B:(h + 1) * OUT_B], acc4[:, :, h, 0:OUT_B],
                                    rden[:, :, h:h + 1].to_broadcast([P, BLOCKS, OUT_B]), ALU.mult)
                link(V.memset(gate[:], 0.0))

                def bc(n):
                    return vec[:, n, :].unsqueeze(1).to_broadcast([P, BLOCKS, K])

                def col(c):
                    return c.unsqueeze(2).to_broadcast([P, BLOCKS, K])

                link(V.tensor_tensor(agg, agg, bc(0), ALU.add))
                mean, var, inv = c_[0][:], c_[1][:], c_[2][:]
                link(V.tensor_reduce(mean, agg, AXX, ALU.add))
                link(V.tensor_scalar(mean, mean, 1.0 / K, None, ALU.mult))
                link(V.tensor_tensor(agg, agg, col(mean), ALU.subtract))
                link(V.tensor_tensor(w_[1][:], agg, agg, ALU.mult))
                link(V.tensor_reduce(var, w_[1][:], AXX, ALU.add))
                V.tensor_scalar(var, var, 1.0 / K, LN_EPS, ALU.mult, ALU.add).then_inc(s_va, 1)
                dve.wait_ge(s_sa, 1)
                link(V.reciprocal(inv, inv))
                link(V.tensor_tensor(agg, agg, col(inv), ALU.mult))
                link(V.tensor_tensor(agg, agg, bc(1), ALU.mult))
                link(V.tensor_tensor(agg, agg, bc(2), ALU.add))
                for e in range(EXPERTS):
                    link(V.tensor_reduce(sc[:, e, :], agg.rearrange("p b (h o) -> p b h o", h=HEADS)[:, :, :, e], AXX, ALU.add))
                link(V.tensor_scalar(sc[:], sc[:], 1.0 / HEADS, None, ALU.mult))
                t = c_[3][:]
                link(V.memset(rank[:], 0.0))
                for e in range(EXPERTS):
                    for o in range(EXPERTS):
                        if o != e:
                            link(V.tensor_tensor(t, sc[:, o, :], sc[:, e, :], ALU.is_ge if o < e else ALU.is_gt))
                            link(V.tensor_tensor(rank[:, e, :], rank[:, e, :], t, ALU.add))
                first, second = c_[4][:], c_[5][:]
                for n, s in enumerate((first, second)):
                    link(V.memset(s, 0.0))
                    for e in range(EXPERTS):
                        link(V.scalar_tensor_tensor(t, rank[:, e, :], float(n), sc[:, e, :], ALU.is_equal, ALU.mult))
                        link(V.tensor_tensor(s, s, t, ALU.add))
                V.tensor_tensor(second, second, first, ALU.subtract).then_inc(s_sub, 1)
                dve.wait_ge(s_exp, 1)
                link(V.tensor_scalar(first, second, 1.0, None, ALU.add))
                link(V.reciprocal(first, first))
                link(V.tensor_tensor(second, second, first, ALU.mult))
                for e in range(EXPERTS):
                    link(V.scalar_tensor_tensor(t, rank[:, e, :], 0.0, first, ALU.is_equal, ALU.mult))
                    link(V.scalar_tensor_tensor(mean, rank[:, e, :], 1.0, second, ALU.is_equal, ALU.mult))
                    link(V.tensor_tensor(gate[:, :, e], t, mean, ALU.add))
                dve.wait_ge(s_w, 16 * (2 * EXPERTS + 1))
                with dve.Fori(0, BLOCKS) as b:
                    link.loop(b, EXPERTS)
                    xb = X[:, bass.ds(b, 1), :].rearrange("p b f -> p (b f)")
                    for e in range(EXPERTS):
                        dve.wait_ge(s_y, b * EXPERTS + (e + 1))
                        link(V.tensor_tensor(y[:, e % 2, :], ps_y[:, e % 2, 0:D], b2b[:, e, :], ALU.add))
                        V.scalar_tensor_tensor(xb, y[:, e % 2, :], gate[:, bass.ds(b, 1), e:e + 1].rearrange("p b e -> p (b e)"),
                                               xb, ALU.mult, ALU.add).then_inc(s_add, 1)
                    link.end(BLOCKS)

            @block.scalar
            def _(act):
                act.wait_ge(s_va, 1)
                nc.scalar.activation(c_[2][:], c_[1][:], ACT.Sqrt).then_inc(s_sa, 1)
                act.wait_ge(s_sub, 1)
                nc.scalar.activation(c_[5][:], c_[5][:], ACT.Exp).then_inc(s_exp, 1)
                act.wait_ge(s_w, 16 * (2 * EXPERTS + 1))

                def gelu(b, e):
                    act.wait_ge(s_hp, b * EXPERTS + (e + 1))
                    if not isinstance(b, int) or b or e >= 2:
                        act.wait_ge(s_y, b * EXPERTS + (e - 1))
                    for c in range(FC):
                        last = nc.scalar.activation(hid[:, e % 2, c, :], ps_h[:, e % 2, c, :], ACT.Gelu, bias=b1c[:, e, c:c + 1])
                    last.then_inc(s_h, 1)

                for e in range(EXPERTS):
                    gelu(0, e)
                with act.Fori(1, BLOCKS) as b:
                    for e in range(EXPERTS):
                        gelu(b, e)

            @block.tensor
            def _(pe):
                pe.wait_ge(s_w1, 16 * EXPERTS)
                pe.wait_ge(s_w, 16 * (2 * EXPERTS + 1))

                def up(b, e):
                    if not isinstance(b, int) or b or e >= 2:
                        pe.wait_ge(s_h, b * EXPERTS + (e - 1))
                    bs = bass.ds(b, 1) if not isinstance(b, int) else slice(b, b + 1)
                    for c in range(FC):
                        for k in range(2):
                            last = nc.tensor.matmul(ps_h[:, e % 2, c, :], w1[:, e, k, c * P:(c + 1) * P],
                                                    A.acc[:, bs, k * P:(k + 1) * P].rearrange("p b n -> p (b n)"),
                                                    start=(k == 0), stop=(k == 1))
                    last.then_inc(s_hp, 1)

                def down(b, e):
                    pe.wait_ge(s_h, b * EXPERTS + (e + 1))
                    if not isinstance(b, int) or b or e >= 2:
                        pe.wait_ge(s_add, b * EXPERTS + (e - 1))
                    for c in range(FC):
                        last = nc.tensor.matmul(ps_y[:, e % 2, 0:D], hid[:, e % 2, c, :], w2[:, e, c, :], start=(c == 0), stop=(c == FC - 1))
                    last.then_inc(s_y, 1)

                def node_block(b, more):
                    for e in range(EXPERTS):
                        if e + 1 < EXPERTS:
                            up(b, e + 1)
                        elif more:
                            up(b + 1, 0)
                        down(b, e)

                up(0, 0)
                node_block(0, True)
                with pe.Fori(1, BLOCKS - 1) as b:
                    node_block(b, True)
                node_block(BLOCKS - 1, False)


_INS = ['x', 'src', 'dst', 'L0_gnn_W', 'L0_gnn_a_src', 'L0_gnn_a_dst', 'L0_ffn_W_gat', 'L0_ffn_att_src',
        'L0_ffn_att_dst', 'L0_ffn_b_gat', 'L0_ffn_ln_gamma', 'L0_ffn_ln_beta', 'L0_ffn_W1', 'L0_ffn_b1',
        'L0_ffn_W2', 'L0_ffn_b2', 'L0_ffn_edge_index']


def kernel(**inputs):
    import numpy as _np
    import concourse.bacc as _bacc
    from concourse import mybir as _mybir
    from concourse.bass_utils import run_bass_kernel_spmd as _run

    nc = _bacc.Bacc("TRN2", target_bir_lowering=False, num_devices=1)
    arrays, args = {}, []
    for name in _INS:
        a = _np.ascontiguousarray(inputs[name])
        arrays[f"in_{name}"] = a
        args.append(nc.dram_tensor(f"in_{name}", a.shape, _mybir.dt.from_np(a.dtype), kind="ExternalInput").ap())
    args.append(nc.dram_tensor("out_0", (N_NODES, D), F32, kind="ExternalOutput").ap())
    build(nc, *args)
    r = _run(nc, [arrays], core_ids=[0])
    return r.results[0]["out_0"]
```

```python
import numpy as np
import concourse.bass as bass
from concourse import mybir
from contextlib import ExitStack

F32 = mybir.dt.float32
BF16 = mybir.dt.bfloat16
I32 = mybir.dt.int32
ALU = mybir.AluOpType
ACT = mybir.ActivationFunctionType
AXX = mybir.AxisListType.X

P = 128
N_NODES = 6250
D = 256
BLOCKS = -(-N_NODES // P)
NPAD = BLOCKS * P
TAIL = N_NODES - (BLOCKS - 1) * P
TRASH = NPAD - 1
NOWHERE = 1 << 20
HEADS = 4
OUT_A = 64
OUT_B = 4
EXPERTS = 4
HID = 512
U = 4
GROUP = U * P
NEG = -1.0e30
LN_EPS = 1e-5
RING = 4


class Graph:

    def __init__(self, name, edges, out, slope):
        self.name = name
        self.edges = edges
        self.cols = -(-edges // P)
        self.out = out
        self.row = HEADS * (out + 1)
        self.slope = slope
        groups = -(-self.cols * P // GROUP) + BLOCKS
        self.groups = -(-groups // RING) * RING
        self.list = self.cols * P


class Chain:

    def __init__(self, eng, sem):
        self.eng, self.sem, self.n, self.i, self.per = eng, sem, 0, None, 0

    def loop(self, i, per):
        self.i, self.per, self.start = i, per, self.n

    def end(self, trips):
        assert self.n - self.start == self.per, (self.n - self.start, self.per)
        self.n = self.start + self.per * trips
        self.i = None

    def mark(self, ins):
        ins.then_inc(self.sem, 1)
        self.n += 1

    def __call__(self, ins):
        self.mark(ins)
        self.wait()

    def wait(self):
        self.eng.wait_ge(self.sem, self.n if self.i is None else self.i * self.per + self.n)


def build(nc, x, src, dst, gnn_W, gnn_a_src, gnn_a_dst, W_gat, att_src, att_dst, b_gat,
          ln_gamma, ln_beta, W1, b1, W2, b2, edge_index, out):
    A = Graph("a", src.shape[0], OUT_A, 0.01)
    B = Graph("b", edge_index.shape[1], OUT_B, 0.2)

    def dram(name, shape, dt):
        return nc.dram_tensor(name, shape, dt, kind="Internal").ap()

    for g in (A, B):
        g.table = dram(f"table_{g.name}", (NPAD, g.row), F32)
        g.ordered = dram(f"ordered_{g.name}", (g.list + GROUP, 2), I32)
        g.plan = dram(f"plan_{g.name}", (3, P * 4), I32)

    ctx = ExitStack()
    with ctx:
        def sb(name, shape, dt=F32, at=ctx):
            return at.enter_context(nc.sbuf_tensor(name, shape, dt))

        def sem(name):
            return ctx.enter_context(nc.semaphore(name))

        X = sb("X", [P, BLOCKS, D])
        ACC = sb("ACC", [P, BLOCKS, A.row])
        ident = sb("ident", [P, P])
        ident_neg = sb("ident_neg", [P, P], BF16)
        iota_row = sb("iota_row", [P, P])
        accB = sb("accB", [P, BLOCKS, B.row])
        for g in (A, B):
            g.ed = sb(f"ed_{g.name}", [P, BLOCKS, HEADS])
            g.mx = sb(f"mx_{g.name}", [P, BLOCKS, HEADS])
        B.pair = sb("pair_b", [P, B.cols, 2], I32)
        B.slot = sb("slot_b", [P, B.cols], I32)
        A.acc, B.acc = ACC, accB

        index_and_nodes(nc, ctx, sb, sem, A, B, X, ident, ident_neg, iota_row,
                        x, src, dst, edge_index, gnn_W, gnn_a_src, gnn_a_dst)
        attend(nc, sem, A, ident, ident_neg, iota_row, B)
        nodes_b(nc, sem, A, B, X, ident, W_gat, att_src, att_dst)
        attend(nc, sem, B, ident, ident_neg, iota_row, None)
        experts(nc, sem, A, B, X, b_gat, ln_gamma, ln_beta, W1, b1, W2, b2, out)


def index_and_nodes(nc, ctx, sb, sem, A, B, X, ident, ident_neg, iota_row,
                    x, src, dst, edge_index, gnn_W, gnn_a_src, gnn_a_dst):
    ph = ExitStack()
    with ph:
        def tb(name, shape, dt=F32):
            return sb(name, shape, dt, ph)

        SC = 4
        T = A.cols
        assert max(A.groups, B.groups) <= 4 * P
        flat = A.acc[:, :, :].rearrange("p b f -> p (b f)")
        dst_i = flat[:, 0:T].bitcast(I32)
        hi = flat[:, T:2 * T]
        mask = flat[:, 2 * T:3 * T]
        scan = flat[:, 3 * T:4 * T]
        pos = flat[:, 4 * T:5 * T]
        part = flat[:, 5 * T:6 * T]
        ones_t = flat[:, 6 * T:7 * T]
        src_i, next_i = pos.bitcast(I32), part.bitcast(I32)
        A.pair = tb("pair_a", [P, A.cols, 2], I32)
        A.slot = tb("slot_a", [P, A.cols], I32)
        for g in (A, B):
            g.rowtot = tb(f"rowtot_{g.name}", [P, BLOCKS])
            g.start = tb(f"start_{g.name}", [P, BLOCKS])
        grp = tb("grp", [P, 4])
        grp_i = tb("grp_i", [P, 3, 4], I32)
        grp_f = tb("grp_f", [P, 3, 4])
        past = tb("past", [P, 2, 4, BLOCKS])
        bad = tb("bad", [P, 1])
        unsorted = tb("unsorted", [P, 1], I32)
        bcol = tb("bcol", [P, BLOCKS])
        ones_mat = tb("ones_mat", [P, P])
        lower = tb("lower", [P, P])
        small = tb("small", [P, 6, BLOCKS])
        small_i = tb("small_i", [P, BLOCKS], I32)
        tail = tb("tail", [P, U, 2], I32)
        stage = tb("stage", [P, 2, SC, 3], I32)
        wx = tb("wx_a", [P, 2, D + 8])
        a_bc = tb("a_bc", [P, 2, D])
        wprod = tb("wprod", [P, 2, D])
        stats = tb("stats", [P, 6])
        mv = tb("mv", [P, 2])
        sd = tb("sd", [P, 2])
        xn = tb("xn", [P, D])
        xt = tb("xt", [P, 2, P])
        ps_cnt = ph.enter_context(nc.psum_tensor("ps_cnt", [P, 512], F32))
        ps_t = ph.enter_context(nc.psum_tensor("ps_t", [P, 2, P], F32))
        ps_z = ph.enter_context(nc.psum_tensor("ps_z", [P, 512], F32))

        s_const = sem("i_const")
        s_idx = sem("i_edges_loaded")
        s_idxb = sem("i_edges_b_loaded")
        s_x = sem("i_x_loaded")
        s_w = sem("i_w_loaded")
        s_fill = sem("i_tails_stored")
        s_fillm = sem("i_tail_made")
        s_plan, s_plans = sem("i_plan_made"), sem("i_plan_stored")
        s_flag, s_list = sem("i_order_known"), sem("i_list_copied")
        s_tot = sem("i_row_totals")
        s_pre = sem("i_prefixes")
        s_rec = sem("i_records")
        s_st = sem("i_staged")
        s_sc = [sem(f"i_scattered{h}") for h in range(2)]
        s_see = sem("i_pool_saw")
        s_dve = sem("i_dve_chain")
        s_zero = sem("i_cleared")
        s_var = sem("i_var")
        s_sd = sem("i_sd")
        s_xn = sem("i_xn")
        s_xtp = sem("i_xt_psum")
        s_xt = sem("i_xt")
        s_z = sem("i_z")
        s_zc = sem("i_z_copied")
        s_seea = sem("i_act_saw")
        s_seev = sem("i_dve_saw")
        s_tab = sem("i_table_stored")
        s_free = sem("i_scratch_free")
        s_pair = sem("i_pairs_made")

        ends = [16 * SC * (-(-(A.cols // SC - h) // 2)) for h in range(2)]
        turns = A.cols // (2 * SC)

        with nc.Block() as block:
            @block.gpsimd
            def _(pool):
                nc.gpsimd.memset(tail[:, :, 0:1], 0).then_inc(s_fillm, 1)
                nc.gpsimd.memset(tail[:, :, 1:2], NOWHERE).then_inc(s_fillm, 1)
                nc.gpsimd.memset(ident[:], 0.0).then_inc(s_const, 1)
                nc.gpsimd.memset(lower[:], 1.0).then_inc(s_const, 1)
                nc.gpsimd.memset(ones_mat[:], 1.0).then_inc(s_const, 1)
                pool.wait_ge(s_const, 3)
                nc.gpsimd.affine_select(out=ident[:], in_=ident[:], compare_op=ALU.not_equal, fill=1.0,
                                        base=0, pattern=[[-1, P]], channel_multiplier=1).then_inc(s_const, 1)
                nc.gpsimd.affine_select(out=lower[:], in_=lower[:], compare_op=ALU.is_gt, fill=0.0,
                                        base=0, pattern=[[1, P]], channel_multiplier=-1).then_inc(s_const, 1)
                nc.gpsimd.iota(iota_row[:], pattern=[[1, P]], base=0, channel_multiplier=0,
                               allow_small_or_imprecise_dtypes=True).then_inc(s_const, 1)
                nc.gpsimd.iota(bcol[:], pattern=[[1, BLOCKS]], base=0, channel_multiplier=0,
                               allow_small_or_imprecise_dtypes=True).then_inc(s_const, 1)
                nc.gpsimd.iota(grp[:], pattern=[[1, 4]], base=0, channel_multiplier=4,
                               allow_small_or_imprecise_dtypes=True).then_inc(s_const, 1)
                pool.wait_ge(s_const, 8)
                pool.wait_ge(s_flag, 1)
                out_of_order = pool.value_load(unsorted[0:1, 0:1], min_val=0, max_val=A.list)
                with pool.If(out_of_order != 0):
                    pool.wait_ge(s_rec, 1)

                    def scatter(i, h):
                        at = i * (2 * SC) + h * SC
                        cols = slice(at, at + SC) if isinstance(i, int) else bass.ds(at, SC)
                        nc.gpsimd.tensor_copy(stage[:, h, :, 0], A.slot[:, cols]).then_inc(s_st, 1)
                        nc.gpsimd.tensor_copy(stage[:, h, :, 1:3], A.pair[:, cols, :]).then_inc(s_st, 1)
                        pool.wait_ge(s_st, i * 4 + (2 * h + 2))
                        pool.sem_inc(s_see, 1)
                        for c in range(SC):
                            pool.indirect_dma_start(
                                out=A.ordered[:, :],
                                out_offset=bass.IndirectOffsetOnAxis(ap=stage[:, h, c, 0:1], axis=0),
                                in_=stage[:, h, c, 1:3], in_offset=None).then_inc(s_sc[h], 16)

                    for h in range(2):
                        scatter(0, h)
                    with pool.Fori(1, turns) as i:
                        for h in range(2):
                            pool.wait_ge(s_sc[h], i * (16 * SC))
                            pool.sem_inc(s_see, 1)
                            scatter(i, h)
                    if A.cols > turns * 2 * SC:
                        assert A.cols == turns * 2 * SC + SC
                        pool.wait_ge(s_sc[0], turns * 16 * SC)
                        scatter(turns, 0)
                    for h in range(2):
                        pool.wait_ge(s_sc[h], ends[h])
                with pool.Else():
                    pool.wait_ge(s_pair, 1)
                    pool.dma_start(A.ordered[0:A.list, :].rearrange("(p t) c -> p (t c)", p=P),
                                   A.pair[:].rearrange("p t c -> p (t c)")).then_inc(s_list, 16)
                    pool.wait_ge(s_list, 16)

            full = A.edges // A.cols
            rest = A.edges - full * A.cols
            assert full < P and rest > 1

            @block.sync
            def _(sp):
                sp.wait_ge(s_zero, 1)
                for tile, first in ((dst_i, 0), (next_i, 1)):
                    sp.dma_start(tile[0:full, :], dst[first:first + full * A.cols].rearrange("(p t) -> p t", t=A.cols)).then_inc(s_idx, 16)
                    sp.dma_start(tile[full:full + 1, 0:rest - first],
                                 dst[first + full * A.cols:A.edges].rearrange("(p t) -> p t", p=1)).then_inc(s_idx, 16)
                sp.dma_start(src_i[0:full, :], src[0:full * A.cols].rearrange("(p t) -> p t", t=A.cols)).then_inc(s_idx, 16)
                sp.dma_start(src_i[full:full + 1, 0:rest], src[full * A.cols:A.edges].rearrange("(p t) -> p t", p=1)).then_inc(s_idx, 16)
                sp.dma_start(X[:, 0:BLOCKS - 1, :], x[0:(BLOCKS - 1) * P, :].rearrange("(b p) f -> p b f", p=P)).then_inc(s_x, 16)
                sp.dma_start(X[0:TAIL, BLOCKS - 1, :], x[(BLOCKS - 1) * P:N_NODES, :]).then_inc(s_x, 16)
                for k in range(2):
                    sp.dma_start(wx[:, k, 0:D].rearrange("p (h o) -> p h o", h=HEADS),
                                 gnn_W[:, k * P:(k + 1) * P, :].rearrange("h p o -> p h o")).then_inc(s_w, 16)
                for n, a in enumerate((gnn_a_src, gnn_a_dst)):
                    sp.dma_start(a_bc[:, n, :], a.rearrange("(u h) o -> u (h o)", u=1).to_broadcast([P, D])).then_inc(s_w, 16)
                sp.wait_ge(s_fillm, 2)
                for g in (A, B):
                    sp.dma_start(g.ordered[g.list:g.list + GROUP, :].rearrange("(p t) c -> p (t c)", p=P),
                                 tail[:].rearrange("p t c -> p (t c)")).then_inc(s_fill, 16)
                sp.wait_ge(s_free, 1)
                for n, t in enumerate((src_i, dst_i)):
                    sp.dma_start(t[:, 0:B.cols], edge_index[n, :].rearrange("(p t) -> p t", t=B.cols)).then_inc(s_idxb, 16)
                for n, g in enumerate((A, B)):
                    sp.wait_ge(s_plan, n + 1)
                    sp.dma_start(g.plan.rearrange("k (p c) -> p k c", p=P), grp_i[:]).then_inc(s_plans, 16)
                    sp.wait_ge(s_plans, 16 * (n + 1))
                sp.wait_ge(s_zc, BLOCKS)
                sp.dma_start(A.table.rearrange("(b p) f -> p b f", p=P), A.acc[:, :, :]).then_inc(s_tab, 16)
                sp.wait_ge(s_tab, 16)
                sp.wait_ge(s_fill, 32)

            @block.vector
            def _(dve):
                link = Chain(dve, s_dve)
                nc.vector.memset(X[:, BLOCKS - 1, :], 0.0)
                nc.vector.memset(dst_i, TRASH)
                nc.vector.memset(next_i, TRASH)
                nc.vector.memset(src_i, 0).then_inc(s_zero, 1)
                link(nc.vector.memset(ones_t, 1.0))
                dve.wait_ge(s_const, 8)
                nc.vector.tensor_scalar(ident_neg[:], ident[:], NEG, None, ALU.mult)

                def blocks_of(g):
                    T = g.cols
                    nc.vector.tensor_scalar(g.pair[:, :, 0], src_i[:, 0:T], N_NODES - 1, None, ALU.min)
                    link(nc.vector.tensor_scalar(g.pair[:, :, 1], dst_i[:, 0:T], TRASH, None, ALU.min))
                    if g is A:
                        link(nc.vector.tensor_scalar(next_i, next_i, TRASH, None, ALU.min))
                        link(nc.vector.tensor_tensor(mask, next_i, g.pair[:, :, 1], ALU.is_lt))
                        link(nc.vector.tensor_reduce(bad[:], mask, AXX, ALU.add))
                    link(nc.vector.tensor_scalar(dst_i[:, 0:T], g.pair[:, :, 1], 7, None, ALU.logical_shift_right))
                    link(nc.vector.tensor_copy(hi[:, 0:T], dst_i[:, 0:T]))
                    with dve.Fori(0, BLOCKS) as b:
                        link.loop(b, 2)
                        link(nc.vector.tensor_scalar(mask[:, 0:T], hi[:, 0:T], bcol[:, bass.ds(b, 1)], None, ALU.is_equal))
                        link(nc.vector.tensor_reduce(g.rowtot[:, bass.ds(b, 1)], mask[:, 0:T], AXX, ALU.add))
                        link.end(BLOCKS)
                    dve.sem_inc(s_tot, 1)

                def plan(g, n):
                    dve.wait_ge(s_pre, n + 1)
                    count, ends_, gcount, gend, gpast, off = [small[:, k, :] for k in range(6)]
                    V = nc.vector
                    link(V.tensor_scalar(small_i[:], ps_cnt[:, 0:BLOCKS], float(GROUP - 1), None, ALU.add))
                    link(V.tensor_scalar(small_i[:], small_i[:], GROUP.bit_length() - 1, None, ALU.logical_shift_right))
                    link(V.tensor_copy(gcount, small_i[:]))
                    link(V.tensor_copy(count, ps_cnt[:, 0:BLOCKS]))
                    link(V.tensor_tensor_scan(gend, ones_t[:, 0:BLOCKS], gcount, 0.0, ALU.mult, ALU.add))
                    link(V.tensor_tensor_scan(ends_, ones_t[:, 0:BLOCKS], count, 0.0, ALU.mult, ALU.add))
                    link(V.tensor_tensor(off, ends_, count, ALU.subtract))
                    link(V.scalar_tensor_tensor(g.start[:], off, 1.0, ps_cnt[:, 64:64 + BLOCKS], ALU.subtract, ALU.add))
                    link(V.tensor_tensor(gpast, gend, gcount, ALU.subtract))
                    link(V.scalar_tensor_tensor(off, gpast, -float(GROUP), off, ALU.mult, ALU.add))
                    link(V.memset(gpast, 0.0))
                    link(V.tensor_tensor(gpast[:, 0:BLOCKS - 1], off[:, 1:BLOCKS], off[:, 0:BLOCKS - 1], ALU.subtract))
                    link(V.tensor_tensor(past[:, 0], grp[:].unsqueeze(2).to_broadcast([P, 4, BLOCKS]),
                                         gend.unsqueeze(1).to_broadcast([P, 4, BLOCKS]), ALU.is_ge))
                    link(V.tensor_tensor(past[:, 1], past[:, 0], gpast.unsqueeze(1).to_broadcast([P, 4, BLOCKS]), ALU.mult))
                    link(V.tensor_reduce(grp_f[:, 0, :], past[:, 0], AXX, ALU.add))
                    link(V.tensor_reduce(grp_f[:, 1, :], past[:, 1], AXX, ALU.add))
                    link(V.tensor_scalar(grp_f[:, 0, :], grp_f[:, 0, :], float(BLOCKS - 1), None, ALU.min))
                    link(V.scalar_tensor_tensor(grp_f[:, 2, :], grp[:], float(GROUP), grp_f[:, 1, :], ALU.mult, ALU.add))
                    if n:
                        dve.wait_ge(s_plans, 16)
                    link(V.tensor_scalar(grp_i[:, 2, :], grp_f[:, 0, :], -float(P), None, ALU.mult))
                    link(V.tensor_copy(grp_i[:, 0, :], grp_f[:, 0, :]))
                    V.tensor_scalar(grp_i[:, 1, :], grp_f[:, 2, :], float(g.list), None, ALU.min).then_inc(s_plan, 1)

                def places(g):
                    T = g.cols
                    link(nc.vector.memset(pos[:, 0:T], 0.0))
                    with dve.Fori(0, BLOCKS) as b:
                        link.loop(b, 4)
                        link(nc.vector.tensor_scalar(mask[:, 0:T], hi[:, 0:T], bcol[:, bass.ds(b, 1)], None, ALU.is_equal))
                        link(nc.vector.tensor_tensor_scan(scan[:, 0:T], ones_t[:, 0:T], mask[:, 0:T], g.start[:, bass.ds(b, 1)], ALU.mult, ALU.add))
                        link(nc.vector.tensor_tensor(part[:, 0:T], mask[:, 0:T], scan[:, 0:T], ALU.mult))
                        link(nc.vector.tensor_tensor(pos[:, 0:T], pos[:, 0:T], part[:, 0:T], ALU.add))
                        link.end(BLOCKS)
                    link(nc.vector.tensor_copy(g.slot[:], pos[:, 0:T]))

                for g in (A, B):
                    nc.vector.memset(g.mx[:], NEG)
                dve.wait_ge(s_idx, 96)
                blocks_of(A)
                dve.sem_inc(s_pair, 1)
                plan(A, 0)
                nc.vector.tensor_scalar(unsorted[:], ps_cnt[:, 128:129], 1.0, None, ALU.mult).then_inc(s_flag, 1)
                dve.wait_ge(s_flag, 1)
                out_of_order = dve.value_load(unsorted[0:1, 0:1], min_val=0, max_val=A.list)
                before = link.n
                with dve.If(out_of_order != 0):
                    places(A)
                    dve.sem_inc(s_rec, 1)
                with dve.Else():
                    dve.sem_inc(s_dve, link.n - before)
                dve.sem_inc(s_free, 1)
                dve.wait_ge(s_idxb, 32)
                blocks_of(B)
                plan(B, 1)
                places(B)

                dve.wait_ge(s_w, 64)
                for k in range(2):
                    for n in range(2):
                        link(nc.vector.tensor_tensor(wprod[:, n, :], wx[:, k, 0:D], a_bc[:, n, :], ALU.mult))
                        link(nc.vector.tensor_reduce(wx[:, k, D + 4 * n:D + 4 * n + 4],
                                                     wprod[:, n, :].rearrange("p (h o) -> p h o", h=HEADS), AXX, ALU.add))
                dve.wait_ge(s_x, 32)
                with dve.Fori(0, BLOCKS) as b:
                    link.loop(b, 3)
                    dve.sem_inc(s_seev, 1)
                    link(nc.vector.bn_stats(stats[:], X[:, bass.ds(b, 1), :].rearrange("p b f -> p (b f)")))
                    dve.sem_inc(s_seev, 1)
                    link(nc.vector.bn_aggr(mv[:], stats[:]))
                    nc.vector.tensor_scalar(sd[:, 0:1], mv[:, 1:2], LN_EPS, None, ALU.add).then_inc(s_var, 1)
                    dve.wait_ge(s_sd, b + 1)
                    link(nc.vector.reciprocal(sd[:, 1:2], sd[:, 1:2]))
                    nc.vector.tensor_scalar(xn[:], X[:, bass.ds(b, 1), :].rearrange("p b f -> p (b f)"), mv[:, 0:1], sd[:, 1:2],
                                            ALU.subtract, ALU.mult).then_inc(s_xn, 1)
                    dve.wait_ge(s_z, b + 1)
                    nc.vector.tensor_scalar(A.acc[:, bass.ds(b, 1), :].rearrange("p b (h o) -> p (b h) o", h=HEADS)[:, :, 0:OUT_A],
                                            ps_z[:, 0:D].rearrange("p (h o) -> p h o", h=HEADS), 1.0, None, ALU.mult)
                    nc.vector.tensor_scalar(A.acc[:, bass.ds(b, 1), :].rearrange("p b (h o) -> p (b h) o", h=HEADS)[:, :, OUT_A],
                                            ps_z[:, D:D + 4], 1.0, None, ALU.mult)
                    nc.vector.tensor_scalar(A.ed[:, bass.ds(b, 1), :].rearrange("p b h -> p (b h)"), ps_z[:, D + 4:D + 8],
                                            1.0, None, ALU.mult).then_inc(s_zc, 1)
                    link.end(BLOCKS)

            @block.scalar
            def _(act):
                with act.Fori(0, BLOCKS) as b:
                    act.wait_ge(s_var, b + 1)
                    nc.scalar.activation(sd[:, 1:2], sd[:, 0:1], ACT.Sqrt).then_inc(s_sd, 1)
                    act.wait_ge(s_xtp, b + 1)
                    nc.scalar.activation(xt[:], ps_t[:], ACT.Copy).then_inc(s_xt, 1)

            @block.tensor
            def _(pe):
                pe.wait_ge(s_const, 8)
                for n, g in enumerate((A, B)):
                    pe.wait_ge(s_tot, n + 1)
                    nc.tensor.matmul(ps_cnt[:, 0:BLOCKS], ones_mat[:], g.rowtot[:], start=True, stop=True)
                    nc.tensor.matmul(ps_cnt[:, 128:129], ones_mat[:], bad[:], start=True, stop=True)
                    nc.tensor.matmul(ps_cnt[:, 64:64 + BLOCKS], lower[:], g.rowtot[:], start=True, stop=True).then_inc(s_pre, 1)
                with pe.Fori(0, BLOCKS) as b:
                    pe.wait_ge(s_xn, b + 1)
                    for k in range(2):
                        last = nc.tensor.transpose(ps_t[:, k, :], xn[:, k * P:(k + 1) * P], ident[:])
                    last.then_inc(s_xtp, 1)
                    pe.wait_ge(s_xt, b + 1)
                    for k in range(2):
                        last = nc.tensor.matmul(ps_z[:, 0:D + 8], xt[:, k, :], wx[:, k, :], start=(k == 0), stop=(k == 1))
                    last.then_inc(s_z, 1)


def attend(nc, sem, g, ident, ident_neg, iota_row, later):
    ph = ExitStack()
    n_ = g.name
    G = g.groups
    with ph:
        def tb(name, shape, dt=F32):
            return ph.enter_context(nc.sbuf_tensor(name + "_" + n_, shape, dt))

        def pt(name, shape):
            return ph.enter_context(nc.psum_tensor(name + "_" + n_, shape, F32))

        o1 = g.out + 1
        dve_tiles = U - 1 if g.out > 16 else U
        blk = tb("blk", [1, 4 * P], I32)
        first = tb("first", [1, 4 * P], I32)
        back = tb("back", [P, 4 * P], I32)
        pair = tb("pair_now", [P, RING, U, 2], I32)
        dl = tb("dl", [P, RING, U], I32)
        if later:
            SC = later.cols // (G // RING)
            extra = later.cols - SC * (G // RING)
            assert extra <= 2 * SC
            stage = tb("stage_sc", [P, max(SC, extra), 3], I32)
        rows = tb("rows", [P, RING, U * HEADS, o1])
        msg = tb("msg", [P, 2, U * HEADS, o1])
        onehot = tb("onehot", [P, RING, U, P])
        other = tb("other", [P, 2, U, P], BF16)
        onehot_t = tb("onehot_t", [P, 2, U, P])
        tmax4 = tb("tmax4", [P, U, HEADS])
        tmax = tb("tmax", [P, 4, HEADS])
        node = tb("node", [P, 2, 2 * HEADS])
        drop = tb("drop", [P, RING, HEADS])
        scale = tb("scale", [P, RING, HEADS])
        u = tb("u", [P, 4, U * HEADS])
        ps_es = pt("ps_es", [P, U, HEADS, P])
        ps_ot = pt("ps_ot", [P, U, P])
        ps_ge = pt("ps_ge", [P, 2, U, 2 * HEADS])
        ps_out = pt("ps_out", [P, 2, 512])

        def sm(name):
            return sem(name + "_" + n_)

        s_plan, s_dl, s_see = sm("plan_loaded"), sm("dl_ready"), sm("pool_saw")
        s_sees = sm("sync_saw")
        s_pair = [sm(f"pairs_loaded{q}") for q in range(RING)]
        s_st, s_sc = sm("scatter_staged"), sm("scattered")
        s_rows = [sm(f"rows_gathered{q}") for q in range(RING)]
        s_oh, s_oth = sm("onehot_ready"), sm("other_ready")
        s_otp, s_ot = sm("onehot_t_psum"), sm("onehot_t_ready")
        s_es, s_mx = sm("scores_spread"), sm("scores_maxed")
        s_drop, s_node, s_scale = sm("drop_ready"), sm("node_ready"), sm("scale_ready")
        s_ge, s_u, s_ex, s_msg = sm("edge_values"), sm("exponent_ready"), sm("weight_ready"), sm("msg_ready")
        s_out, s_acc = sm("sums_ready"), sm("sums_added")
        s_msga = sm("msg_by_act_ready")
        s_dve = sm("dve_chain")
        trips = G // RING - 1

        def steps(eng, step):
            for it in range(RING):
                step(it, it, it >= 1, it >= 2, True)
            with eng.Fori(0, trips) as i:
                yield i
                for v in range(RING):
                    step(i * RING + (RING + v), v, True, True, True)
            step(G, 0, True, True, False)
            step(G + 1, 1, False, True, False)

        with nc.Block() as block:
            @block.sync
            def _(sp):
                sp.dma_start(blk[:], g.plan[0:1, :]).then_inc(s_plan, 16)
                sp.dma_start(first[:], g.plan[1:2, :]).then_inc(s_plan, 16)
                sp.dma_start(back[:], g.plan[2:3, :].to_broadcast([P, 4 * P])).then_inc(s_plan, 16)
                sp.wait_ge(s_plan, 48)

                def load(grp, q):
                    c = slice(grp, grp + 1) if isinstance(grp, int) else bass.ds(grp, 1)
                    e = sp.value_load(first[0:1, c], min_val=0, max_val=g.list)
                    sp.dma_start(pair[:, q].rearrange("p j c -> p (j c)"),
                                 g.ordered[bass.ds(e, GROUP), :].rearrange("(p j) c -> p (j c)", p=P)).then_inc(s_pair[q], 16)

                for q in range(RING):
                    load(q, q)
                with sp.Fori(0, trips) as i:
                    for q in range(RING):
                        sp.wait_ge(s_rows[q], (i + 1) * (16 * U))
                        sp.sem_inc(s_sees, 1)
                        sp.wait_ge(s_dl, i * RING + (q + 1))
                        sp.sem_inc(s_sees, 1)
                        load(i * RING + (RING + q), q)

            @block.gpsimd
            def _(pool):
                pool.wait_ge(s_plan, 48)

                def gather(i, q):
                    grp = i * RING + q
                    c = slice(grp, grp + 1) if isinstance(grp, int) else bass.ds(grp, 1)
                    pool.wait_ge(s_pair[q], i * 16 + 16)
                    if not isinstance(i, int):
                        pool.wait_ge(s_oh, i * RING + (q + 1 - RING))
                    pool.sem_inc(s_see, 1)
                    nc.gpsimd.tensor_tensor(dl[:, q, :], pair[:, q, :, 1], back[:, c].to_broadcast([P, U]), ALU.add).then_inc(s_dl, 1)
                    if not isinstance(i, int):
                        pool.wait_ge(s_msg, i * RING + (q + 1 - RING))
                        if dve_tiles < U:
                            pool.wait_ge(s_msga, i * RING + (q + 1 - RING))
                        pool.sem_inc(s_see, 1)
                    for j in range(U):
                        pool.indirect_dma_start(
                            out=rows[:, q, j * HEADS:(j + 1) * HEADS, :].rearrange("p h o -> p (h o)"), out_offset=None,
                            in_=g.table[:, :],
                            in_offset=bass.IndirectOffsetOnAxis(ap=pair[:, q, j, 0:1], axis=0)).then_inc(s_rows[q], 16)

                def stage_columns(first_col, n, turn):
                    if not isinstance(turn, int) or turn:
                        pool.wait_ge(s_sc, turn * (16 * SC))
                        pool.sem_inc(s_see, 1)
                    c = slice(first_col, first_col + n) if isinstance(first_col, int) else bass.ds(first_col, n)
                    nc.gpsimd.tensor_copy(stage[:, 0:n, 0], later.slot[:, c]).then_inc(s_st, 1)
                    nc.gpsimd.tensor_copy(stage[:, 0:n, 1:3], later.pair[:, c, :]).then_inc(s_st, 1)
                    pool.wait_ge(s_st, turn * 2 + 2)
                    pool.sem_inc(s_see, 1)

                def scatter(c):
                    pool.indirect_dma_start(
                        out=later.ordered[:, :],
                        out_offset=bass.IndirectOffsetOnAxis(ap=stage[:, c, 0:1], axis=0),
                        in_=stage[:, c, 1:3], in_offset=None).then_inc(s_sc, 16)

                def turn(i):
                    if later:
                        stage_columns(i * SC, SC, i)
                    for q in range(RING):
                        gather(i, q)
                        if later:
                            for c in range(q * SC // (RING - 1), min(SC, (q + 1) * SC // (RING - 1))):
                                scatter(c)

                turn(0)
                with pool.Fori(1, trips + 1) as i:
                    turn(i)
                pool.wait_ge(s_oh, G)
                pool.sem_inc(s_dl, 1)
                if later:
                    turns = G // RING
                    if extra:
                        stage_columns(turns * SC, extra, turns)
                        for c in range(extra):
                            scatter(c)
                    pool.wait_ge(s_sc, 16 * later.cols)

            @block.vector
            def _(dve):
                link = Chain(dve, s_dve)
                dve.wait_ge(s_plan, 48)
                if g.name == "a":
                    nc.vector.memset(g.acc[:, :, :], 0.0)

                def make_onehot(it, q):
                    if not isinstance(it, int) or it >= RING:
                        dve.wait_ge(s_out, it - (RING - 1))
                    dve.wait_ge(s_dl, it + 1)
                    nc.vector.tensor_tensor(onehot[:, q], iota_row[:].unsqueeze(1).to_broadcast([P, U, P]),
                                            dl[:, q, :].unsqueeze(2).to_broadcast([P, U, P]), ALU.is_equal).then_inc(s_oh, 1)

                def block_of(grp):
                    c = bass.ds(grp, 1) if not isinstance(grp, int) else slice(grp, grp + 1)
                    return dve.value_load(blk[0:1, c], min_val=0, max_val=BLOCKS - 1)

                def at(t, b):
                    return t[:, bass.ds(b, 1), :].rearrange("p b f -> p (b f)")

                def step(it, q, prev, prev2, now):
                    static = isinstance(it, int)
                    p, r = (q - 1) % 2, (q - 1) % RING
                    p2, r2 = q % 2, (q - 2) % RING
                    new = node[:, q % 2, :]
                    if now:
                        make_onehot(it + 1, (q + 1) % RING)
                        for j in range(U):
                            if j == 2:
                                b = block_of(it)
                            if j == 3 and prev2:
                                b2 = block_of(it - 2)
                            dve.wait_ge(s_es, it * U + (j + 1))
                            nc.vector.tensor_reduce(tmax4[:, j, :], ps_es[:, j], AXX, ALU.max).then_inc(s_mx, 1)
                    if prev2:
                        if not now:
                            b2 = block_of(it - 2)
                        a = g.acc[:, bass.ds(b2, 1), :].rearrange("p b (h o) -> p (b h) o", h=HEADS)
                        dve.wait_ge(s_scale, it - 1)
                        if not static or it >= 3:
                            dve.wait_ge(s_acc, it - 2)
                        link.mark(nc.vector.tensor_tensor(a, a, scale[:, r2, :].unsqueeze(2).to_broadcast([P, HEADS, o1]), ALU.mult))
                    if now:
                        dve.wait_ge(s_mx, it * U + U)
                        link.mark(nc.vector.tensor_reduce(tmax[:, 0, :], tmax4[:].rearrange("p j h -> p h j"), AXX, ALU.max))
                    if prev:
                        dve.wait_ge(s_ge, it)
                        u4 = [u[:, n, :].rearrange("p (j h) -> p j h", j=U) for n in range(3)]
                        link.mark(nc.vector.tensor_tensor(u4[0], ps_ge[:, p, :, 0:HEADS],
                                                          rows[:, r, :, g.out].rearrange("p (j h) -> p j h", j=U), ALU.add))
                    link.wait()
                    if now:
                        link.mark(nc.vector.tensor_tensor(tmax[:, 1, :], tmax[:, 0, :], at(g.ed, b), ALU.add))
                    if prev:
                        link.mark(nc.vector.scalar_tensor_tensor(u[:, 1, :], u[:, 0, :], g.slope, u[:, 0, :], ALU.mult, ALU.max))
                        link.wait()
                        link.mark(nc.vector.tensor_tensor(u4[2], u4[1], ps_ge[:, p, :, HEADS:], ALU.subtract))
                    if now:
                        if not prev:
                            link.wait()
                        link.mark(nc.vector.scalar_tensor_tensor(tmax[:, 2, :], tmax[:, 1, :], g.slope, tmax[:, 1, :], ALU.mult, ALU.max))
                    link.wait()
                    if prev:
                        nc.vector.tensor_scalar(u[:, 3, :], u[:, 2, :], 0.0, None, ALU.min).then_inc(s_u, 1)
                    if now:
                        link(nc.vector.tensor_tensor(new[:, HEADS:], tmax[:, 2, :], at(g.mx, b), ALU.max))
                        nc.vector.tensor_tensor(drop[:, q, :], at(g.mx, b), new[:, HEADS:], ALU.subtract).then_inc(s_drop, 1)
                        nc.vector.tensor_scalar(new[:, 0:HEADS], at(g.ed, b), 1.0, None, ALU.mult).then_inc(s_node, 1)
                        dve.wait_ge(s_drop, it + 1)
                        link.mark(nc.vector.tensor_scalar(at(g.mx, b), new[:, HEADS:], 1.0, None, ALU.mult))
                    if prev:
                        dve.wait_ge(s_ex, it)
                        mine = slice(0, dve_tiles * HEADS)
                        nc.vector.tensor_tensor(msg[:, p, mine, 0:g.out], rows[:, r, mine, 0:g.out],
                                                msg[:, p, mine, g.out:].to_broadcast([P, dve_tiles * HEADS, g.out]),
                                                ALU.mult).then_inc(s_msg, 1)
                    link.wait()
                    if prev2:
                        dve.wait_ge(s_out, it - 1)
                        nc.vector.tensor_tensor(a, a, ps_out[:, p2, 0:g.row].rearrange("p (h o) -> p h o", h=HEADS), ALU.add).then_inc(s_acc, 1)

                make_onehot(0, 0)
                for it in range(RING):
                    step(it, it, it >= 1, it >= 2, True)
                with dve.Fori(0, trips) as i:
                    link.loop(i, RING * 9)
                    for v in range(RING):
                        step(i * RING + (RING + v), v, True, True, True)
                    link.end(trips)
                step(G, 0, True, True, False)
                step(G + 1, 1, False, True, False)

            @block.scalar
            def _(act):
                def other_of(it, q):
                    act.wait_ge(s_oh, it + 1)
                    if not isinstance(it, int) or it >= 2:
                        act.wait_ge(s_es, it * U - U)
                    nc.scalar.activation(other[:, q % 2], onehot[:, q], ACT.Identity, bias=1.0, scale=-1.0).then_inc(s_oth, 1)

                def step(it, q, prev, prev2, now):
                    static = isinstance(it, int)
                    if now:
                        act.wait_ge(s_otp, it + 1)
                        if not static or it >= 2:
                            act.wait_ge(s_ge, it - 1)
                        nc.scalar.activation(onehot_t[:, q % 2], ps_ot[:], ACT.Copy).then_inc(s_ot, 1)
                        other_of(it + 1, (q + 1) % RING)
                        act.wait_ge(s_drop, it + 1)
                        if not static or it >= RING:
                            act.wait_ge(s_acc, it - (RING - 1))
                        nc.scalar.activation(scale[:, q, :], drop[:, q, :], ACT.Exp).then_inc(s_scale, 1)
                    if prev:
                        act.wait_ge(s_u, it)
                        if not static or it >= 3:
                            act.wait_ge(s_out, it - 2)
                        p, r = (q - 1) % 2, (q - 1) % RING
                        nc.scalar.activation(msg[:, p, :, g.out], u[:, 3, :], ACT.Exp).then_inc(s_ex, 1)
                        act.wait_ge(s_ex, it)
                        for n in range(dve_tiles * HEADS, U * HEADS):
                            last = nc.scalar.activation(msg[:, p, n, 0:g.out], rows[:, r, n, 0:g.out], ACT.Copy,
                                                        scale=msg[:, p, n, g.out:])
                            if n == U * HEADS - 1:
                                last.then_inc(s_msga, 1)

                other_of(0, 0)
                for it in range(RING):
                    step(it, it, it >= 1, it >= 2, True)
                with act.Fori(0, trips) as i:
                    for v in range(RING):
                        step(i * RING + (RING + v), v, True, True, True)
                step(G, 0, True, True, False)

            @block.tensor
            def _(pe):
                def step(it, i, q, prev, prev2, now):
                    static = isinstance(it, int)
                    if now:
                        pe.wait_ge(s_oth, it + 1)
                        if not static or it >= 1:
                            pe.wait_ge(s_ot, it)
                        for j in range(U):
                            last = nc.tensor.transpose(ps_ot[:, j, :], onehot[:, q, j, :], ident[:])
                        last.then_inc(s_otp, 1)
                        pe.wait_ge(s_rows[q], (i + 1) * (16 * U))
                        for j in range(U):
                            if not static or it >= 1:
                                pe.wait_ge(s_mx, it * U + (j + 1 - U))
                            for h in range(HEADS):
                                nc.tensor.matmul(ps_es[:, j, h, :], rows[:, q, j * HEADS + h, g.out:].to_broadcast([P, P]),
                                                 ident[:], start=(h == 0), stop=False, is_transpose=True)
                            nc.tensor.matmul(ps_es[:, j], other[:, q % 2, j, :],
                                             ident_neg[:].unsqueeze(1).to_broadcast([P, HEADS, P]),
                                             start=False, stop=True).then_inc(s_es, 1)
                    if prev:
                        p = (q - 1) % 2
                        pe.wait_ge(s_ot, it)
                        pe.wait_ge(s_node, it)
                        if not static or it >= 2:
                            pe.wait_ge(s_u, it - 1)
                        for j in range(U):
                            last = nc.tensor.matmul(ps_ge[:, p, j, :], onehot_t[:, p, j, :], node[:, p, :], start=True, stop=True)
                        last.then_inc(s_ge, 1)
                    if prev2:
                        p, r = q % 2, (q - 2) % RING
                        pe.wait_ge(s_ex, it - 1)
                        pe.wait_ge(s_msg, it - 1)
                        if dve_tiles < U:
                            pe.wait_ge(s_msga, it - 1)
                        if not static or it >= 4:
                            pe.wait_ge(s_acc, it - 3)
                        for j in range(U):
                            last = nc.tensor.matmul(ps_out[:, p, 0:g.row], onehot[:, r, j, :],
                                                    msg[:, p, j * HEADS:(j + 1) * HEADS, :].rearrange("p h o -> p (h o)"),
                                                    start=(j == 0), stop=(j == U - 1))
                        last.then_inc(s_out, 1)

                for it in range(RING):
                    step(it, 0, it, it >= 1, it >= 2, True)
                with pe.Fori(0, trips) as i:
                    for v in range(RING):
                        step(i * RING + (RING + v), i + 1, v, True, True, True)
                step(G, 0, 0, True, True, False)
                step(G + 1, 0, 1, False, True, False)


def nodes_b(nc, sem, A, B, X, ident, W_gat, att_src, att_dst):
    ph = ExitStack()
    with ph:
        def tb(name, shape, dt=F32):
            return ph.enter_context(nc.sbuf_tensor("nb_" + name, shape, dt))

        K = HEADS * OUT_B
        wx = tb("wx", [P, 2, K + 8])
        a_bc = tb("a_bc", [P, 2, K])
        wprod = tb("wprod", [P, 2, K])
        rden = tb("rden", [P, 2, HEADS])
        add = tb("add", [P, D])
        stats = tb("stats", [P, 6])
        mv = tb("mv", [P, 2])
        sd = tb("sd", [P, 2])
        xn = tb("xn", [P, D])
        xt = tb("xt", [P, 2, P])
        rowsB = tb("rows", [P, BLOCKS, B.row])
        selfs = tb("self", [P, BLOCKS, HEADS])
        ps_t = ph.enter_context(nc.psum_tensor("nb_ps_t", [P, 2, P], F32))
        ps_z = ph.enter_context(nc.psum_tensor("nb_ps_z", [P, 512], F32))
        s_w = sem("nb_w_loaded")
        s_dve = sem("nb_dve_chain")
        s_seev = sem("nb_dve_saw")
        s_var, s_sd, s_xn = sem("nb_var"), sem("nb_sd"), sem("nb_xn")
        s_xtp, s_xt, s_z, s_zc = sem("nb_xt_psum"), sem("nb_xt"), sem("nb_z"), sem("nb_z_copied")
        s_tab = sem("nb_table_stored")
        with nc.Block() as block:
            @block.sync
            def _(sp):
                sp.dma_start(wx[:, :, 0:K], W_gat.rearrange("(k p) f -> p k f", p=P)).then_inc(s_w, 16)
                for n, a in enumerate((att_src, att_dst)):
                    sp.dma_start(a_bc[:, n, :], a.rearrange("(u h) o -> u (h o)", u=1).to_broadcast([P, K])).then_inc(s_w, 16)
                sp.wait_ge(s_zc, BLOCKS)
                sp.dma_start(B.table.rearrange("(b p) f -> p b f", p=P), rowsB[:]).then_inc(s_tab, 16)
                sp.wait_ge(s_tab, 16)

            @block.vector
            def _(dve):
                link = Chain(dve, s_dve)
                dve.wait_ge(s_w, 48)
                for k in range(2):
                    for n in range(2):
                        link(nc.vector.tensor_tensor(wprod[:, n, :], wx[:, k, 0:K], a_bc[:, n, :], ALU.mult))
                        link(nc.vector.tensor_reduce(wx[:, k, K + 4 * n:K + 4 * n + 4],
                                                     wprod[:, n, :].rearrange("p (h o) -> p h o", h=HEADS), AXX, ALU.add))
                with dve.Fori(0, BLOCKS) as b:
                    link.loop(b, 7)
                    xb = X[:, bass.ds(b, 1), :].rearrange("p b f -> p (b f)")
                    ab = A.acc[:, bass.ds(b, 1), :].rearrange("p b (h o) -> p (b h) o", h=HEADS)
                    link(nc.vector.tensor_scalar(rden[:, 0, :], ab[:, :, OUT_A], 1e-30, None, ALU.max))
                    link(nc.vector.reciprocal(rden[:, 1, :], rden[:, 0, :]))
                    link(nc.vector.tensor_tensor(add[:].rearrange("p (h o) -> p h o", h=HEADS), ab[:, :, 0:OUT_A],
                                                 rden[:, 1, :].unsqueeze(2).to_broadcast([P, HEADS, OUT_A]), ALU.mult))
                    link(nc.vector.tensor_tensor(xb, xb, add[:], ALU.add))
                    dve.sem_inc(s_seev, 1)
                    link(nc.vector.bn_stats(stats[:], xb))
                    dve.sem_inc(s_seev, 1)
                    link(nc.vector.bn_aggr(mv[:], stats[:]))
                    nc.vector.tensor_scalar(sd[:, 0:1], mv[:, 1:2], LN_EPS, None, ALU.add).then_inc(s_var, 1)
                    dve.wait_ge(s_sd, b + 1)
                    link(nc.vector.reciprocal(sd[:, 1:2], sd[:, 1:2]))
                    nc.vector.tensor_scalar(xn[:], xb, mv[:, 0:1], sd[:, 1:2], ALU.subtract, ALU.mult).then_inc(s_xn, 1)
                    dve.wait_ge(s_xt, b + 1)
                    nc.vector.tensor_scalar(A.acc[:, bass.ds(b, 1), 0:D].rearrange("p b f -> p (b f)"),
                                            xt[:].rearrange("p k n -> p (k n)"), 1.0, None, ALU.mult)
                    dve.wait_ge(s_z, b + 1)
                    rb = rowsB[:, bass.ds(b, 1), :].rearrange("p b (h o) -> p (b h) o", h=HEADS)
                    nc.vector.tensor_scalar(rb[:, :, 0:OUT_B], ps_z[:, 0:K].rearrange("p (h o) -> p h o", h=HEADS), 1.0, None, ALU.mult)
                    nc.vector.tensor_scalar(rb[:, :, OUT_B], ps_z[:, K:K + 4], 1.0, None, ALU.mult)
                    nc.vector.tensor_scalar(B.ed[:, bass.ds(b, 1), :].rearrange("p b h -> p (b h)"), ps_z[:, K + 4:K + 8],
                                            1.0, None, ALU.mult).then_inc(s_zc, 1)
                    link.end(BLOCKS)
                dve.wait_ge(s_zc, BLOCKS)
                rows4 = rowsB[:].rearrange("p b (h o) -> p b h o", h=HEADS)
                link(nc.vector.tensor_copy(B.acc[:, :, :], rowsB[:]))
                nc.vector.memset(B.acc[:, :, :].rearrange("p b (h o) -> p b h o", h=HEADS)[:, :, :, OUT_B], 1.0)
                link(nc.vector.tensor_tensor(selfs[:], rows4[:, :, :, OUT_B], B.ed[:, :, :], ALU.add))
                nc.vector.scalar_tensor_tensor(B.mx[:, :, :], selfs[:], B.slope, selfs[:], ALU.mult, ALU.max)

            @block.scalar
            def _(act):
                with act.Fori(0, BLOCKS) as b:
                    act.wait_ge(s_var, b + 1)
                    nc.scalar.activation(sd[:, 1:2], sd[:, 0:1], ACT.Sqrt).then_inc(s_sd, 1)
                    act.wait_ge(s_xtp, b + 1)
                    nc.scalar.activation(xt[:], ps_t[:], ACT.Copy).then_inc(s_xt, 1)

            @block.tensor
            def _(pe):
                with pe.Fori(0, BLOCKS) as b:
                    pe.wait_ge(s_xn, b + 1)
                    for k in range(2):
                        last = nc.tensor.transpose(ps_t[:, k, :], xn[:, k * P:(k + 1) * P], ident[:])
                    last.then_inc(s_xtp, 1)
                    pe.wait_ge(s_xt, b + 1)
                    for k in range(2):
                        last = nc.tensor.matmul(ps_z[:, 0:K + 8], xt[:, k, :], wx[:, k, :], start=(k == 0), stop=(k == 1))
                    last.then_inc(s_z, 1)


def experts(nc, sem, A, B, X, b_gat, ln_gamma, ln_beta, W1, b1, W2, b2, out):
    ph = ExitStack()
    with ph:
        def tb(name, shape, dt=F32):
            return ph.enter_context(nc.sbuf_tensor("ex_" + name, shape, dt))

        K = HEADS * OUT_B
        FC = HID // P
        w1 = tb("w1", [P, EXPERTS, 2, HID])
        w2 = tb("w2", [P, EXPERTS, FC, D])
        b1c = tb("b1c", [P, EXPERTS, FC])
        b2b = tb("b2b", [P, EXPERTS, D])
        vec = tb("vec", [P, 3, K])
        w_ = [tb(f"wk{i}", [P, BLOCKS, K]) for i in range(2)]
        c_ = [tb(f"ck{i}", [P, BLOCKS]) for i in range(6)]
        rden = tb("rden", [P, BLOCKS, HEADS])
        sc = tb("sc", [P, EXPERTS, BLOCKS])
        rank = tb("rank", [P, EXPERTS, BLOCKS])
        gate = tb("gate", [P, BLOCKS, EXPERTS])
        hid = tb("hid", [P, 2, FC, P])
        y = tb("y", [P, 2, D])
        ps_h = ph.enter_context(nc.psum_tensor("ex_ps_h", [P, 2, FC, P], F32))
        ps_y = ph.enter_context(nc.psum_tensor("ex_ps_y", [P, 2, 512], F32))
        s_w, s_w1, s_v = sem("ex_w_loaded"), sem("ex_w1_loaded"), sem("ex_vectors_loaded")
        s_dve, s_va, s_sa, s_sub, s_exp = sem("ex_dve_chain"), sem("ex_var"), sem("ex_std"), sem("ex_sub"), sem("ex_exp")
        s_hp, s_h, s_y, s_add, s_o = sem("ex_hidden_psum"), sem("ex_hidden"), sem("ex_y"), sem("ex_added"), sem("ex_stored")
        with nc.Block() as block:
            @block.sync
            def _(sp):
                for e in range(EXPERTS):
                    sp.dma_start(w1[:, e], W1[e].rearrange("(k p) f -> p k f", p=P)).then_inc(s_w1, 16)
                for e in range(EXPERTS):
                    sp.dma_start(b1c[:, e, :], b1[e:e + 1, :].rearrange("u (c p) -> p (u c)", p=P), allow_slow_non_contiguous=True).then_inc(s_w, 16)
                    sp.dma_start(w2[:, e], W2[e].rearrange("(c p) f -> p c f", p=P)).then_inc(s_w, 16)
                sp.dma_start(b2b[:].rearrange("p e f -> p (e f)"), b2.rearrange("(u e) f -> u (e f)", u=1).to_broadcast([P, EXPERTS * D])).then_inc(s_w, 16)
                for n, v in enumerate((b_gat, ln_gamma, ln_beta)):
                    sp.dma_start(vec[:, n, :], v.rearrange("(u f) -> u f", u=1).to_broadcast([P, K])).then_inc(s_v, 16)
                sp.wait_ge(s_add, BLOCKS * EXPERTS)
                sp.dma_start(out[0:(BLOCKS - 1) * P, :].rearrange("(b p) f -> p b f", p=P), X[:, 0:BLOCKS - 1, :]).then_inc(s_o, 16)
                sp.dma_start(out[(BLOCKS - 1) * P:N_NODES, :], X[0:TAIL, BLOCKS - 1, :]).then_inc(s_o, 16)
                sp.wait_ge(s_o, 32)

            @block.vector
            def _(dve):
                link = Chain(dve, s_dve)
                V = nc.vector
                dve.wait_ge(s_v, 48)
                acc4 = B.acc[:, :, :].rearrange("p b (h o) -> p b h o", h=HEADS)
                link(V.tensor_scalar(rden[:], acc4[:, :, :, OUT_B], 1e-16, None, ALU.add))
                link(V.reciprocal(rden[:], rden[:]))
                agg = w_[0][:]
                for h in range(HEADS):
                    V.tensor_tensor(agg[:, :, h * OUT_B:(h + 1) * OUT_B], acc4[:, :, h, 0:OUT_B],
                                    rden[:, :, h:h + 1].to_broadcast([P, BLOCKS, OUT_B]), ALU.mult)
                link(V.memset(gate[:], 0.0))

                def bc(n):
                    return vec[:, n, :].unsqueeze(1).to_broadcast([P, BLOCKS, K])

                def col(c):
                    return c.unsqueeze(2).to_broadcast([P, BLOCKS, K])

                link(V.tensor_tensor(agg, agg, bc(0), ALU.add))
                mean, var, inv = c_[0][:], c_[1][:], c_[2][:]
                link(V.tensor_reduce(mean, agg, AXX, ALU.add))
                link(V.tensor_scalar(mean, mean, 1.0 / K, None, ALU.mult))
                link(V.tensor_tensor(agg, agg, col(mean), ALU.subtract))
                link(V.tensor_tensor(w_[1][:], agg, agg, ALU.mult))
                link(V.tensor_reduce(var, w_[1][:], AXX, ALU.add))
                V.tensor_scalar(var, var, 1.0 / K, LN_EPS, ALU.mult, ALU.add).then_inc(s_va, 1)
                dve.wait_ge(s_sa, 1)
                link(V.reciprocal(inv, inv))
                link(V.tensor_tensor(agg, agg, col(inv), ALU.mult))
                link(V.tensor_tensor(agg, agg, bc(1), ALU.mult))
                link(V.tensor_tensor(agg, agg, bc(2), ALU.add))
                for e in range(EXPERTS):
                    link(V.tensor_reduce(sc[:, e, :], agg.rearrange("p b (h o) -> p b h o", h=HEADS)[:, :, :, e], AXX, ALU.add))
                link(V.tensor_scalar(sc[:], sc[:], 1.0 / HEADS, None, ALU.mult))
                t = c_[3][:]
                link(V.memset(rank[:], 0.0))
                for e in range(EXPERTS):
                    for o in range(EXPERTS):
                        if o != e:
                            link(V.tensor_tensor(t, sc[:, o, :], sc[:, e, :], ALU.is_ge if o < e else ALU.is_gt))
                            link(V.tensor_tensor(rank[:, e, :], rank[:, e, :], t, ALU.add))
                first, second = c_[4][:], c_[5][:]
                for n, s in enumerate((first, second)):
                    link(V.memset(s, 0.0))
                    for e in range(EXPERTS):
                        link(V.scalar_tensor_tensor(t, rank[:, e, :], float(n), sc[:, e, :], ALU.is_equal, ALU.mult))
                        link(V.tensor_tensor(s, s, t, ALU.add))
                V.tensor_tensor(second, second, first, ALU.subtract).then_inc(s_sub, 1)
                dve.wait_ge(s_exp, 1)
                link(V.tensor_scalar(first, second, 1.0, None, ALU.add))
                link(V.reciprocal(first, first))
                link(V.tensor_tensor(second, second, first, ALU.mult))
                for e in range(EXPERTS):
                    link(V.scalar_tensor_tensor(t, rank[:, e, :], 0.0, first, ALU.is_equal, ALU.mult))
                    link(V.scalar_tensor_tensor(mean, rank[:, e, :], 1.0, second, ALU.is_equal, ALU.mult))
                    link(V.tensor_tensor(gate[:, :, e], t, mean, ALU.add))
                dve.wait_ge(s_w, 16 * (2 * EXPERTS + 1))
                with dve.Fori(0, BLOCKS) as b:
                    link.loop(b, EXPERTS)
                    xb = X[:, bass.ds(b, 1), :].rearrange("p b f -> p (b f)")
                    for e in range(EXPERTS):
                        dve.wait_ge(s_y, b * EXPERTS + (e + 1))
                        link(V.tensor_tensor(y[:, e % 2, :], ps_y[:, e % 2, 0:D], b2b[:, e, :], ALU.add))
                        V.scalar_tensor_tensor(xb, y[:, e % 2, :], gate[:, bass.ds(b, 1), e:e + 1].rearrange("p b e -> p (b e)"),
                                               xb, ALU.mult, ALU.add).then_inc(s_add, 1)
                    link.end(BLOCKS)

            @block.scalar
            def _(act):
                act.wait_ge(s_va, 1)
                nc.scalar.activation(c_[2][:], c_[1][:], ACT.Sqrt).then_inc(s_sa, 1)
                act.wait_ge(s_sub, 1)
                nc.scalar.activation(c_[5][:], c_[5][:], ACT.Exp).then_inc(s_exp, 1)
                act.wait_ge(s_w, 16 * (2 * EXPERTS + 1))

                def gelu(b, e):
                    act.wait_ge(s_hp, b * EXPERTS + (e + 1))
                    if not isinstance(b, int) or b or e >= 2:
                        act.wait_ge(s_y, b * EXPERTS + (e - 1))
                    for c in range(FC):
                        last = nc.scalar.activation(hid[:, e % 2, c, :], ps_h[:, e % 2, c, :], ACT.Gelu, bias=b1c[:, e, c:c + 1])
                    last.then_inc(s_h, 1)

                for e in range(EXPERTS):
                    gelu(0, e)
                with act.Fori(1, BLOCKS) as b:
                    for e in range(EXPERTS):
                        gelu(b, e)

            @block.tensor
            def _(pe):
                pe.wait_ge(s_w1, 16 * EXPERTS)
                pe.wait_ge(s_w, 16 * (2 * EXPERTS + 1))

                def up(b, e):
                    if not isinstance(b, int) or b or e >= 2:
                        pe.wait_ge(s_h, b * EXPERTS + (e - 1))
                    bs = bass.ds(b, 1) if not isinstance(b, int) else slice(b, b + 1)
                    for c in range(FC):
                        for k in range(2):
                            last = nc.tensor.matmul(ps_h[:, e % 2, c, :], w1[:, e, k, c * P:(c + 1) * P],
                                                    A.acc[:, bs, k * P:(k + 1) * P].rearrange("p b n -> p (b n)"),
                                                    start=(k == 0), stop=(k == 1))
                    last.then_inc(s_hp, 1)

                def down(b, e):
                    pe.wait_ge(s_h, b * EXPERTS + (e + 1))
                    if not isinstance(b, int) or b or e >= 2:
                        pe.wait_ge(s_add, b * EXPERTS + (e - 1))
                    for c in range(FC):
                        last = nc.tensor.matmul(ps_y[:, e % 2, 0:D], hid[:, e % 2, c, :], w2[:, e, c, :], start=(c == 0), stop=(c == FC - 1))
                    last.then_inc(s_y, 1)

                def node_block(b, more):
                    for e in range(EXPERTS):
                        if e + 1 < EXPERTS:
                            up(b, e + 1)
                        elif more:
                            up(b + 1, 0)
                        down(b, e)

                up(0, 0)
                node_block(0, True)
                with pe.Fori(1, BLOCKS - 1) as b:
                    node_block(b, True)
                node_block(BLOCKS - 1, False)


_INS = ['x', 'src', 'dst', 'L0_gnn_W', 'L0_gnn_a_src', 'L0_gnn_a_dst', 'L0_ffn_W_gat', 'L0_ffn_att_src',
        'L0_ffn_att_dst', 'L0_ffn_b_gat', 'L0_ffn_ln_gamma', 'L0_ffn_ln_beta', 'L0_ffn_W1', 'L0_ffn_b1',
        'L0_ffn_W2', 'L0_ffn_b2', 'L0_ffn_edge_index']


def kernel(**inputs):
    import numpy as _np
    import concourse.bacc as _bacc
    from concourse import mybir as _mybir
    from concourse.bass_utils import run_bass_kernel_spmd as _run

    nc = _bacc.Bacc("TRN2", target_bir_lowering=False, num_devices=1)
    arrays, args = {}, []
    for name in _INS:
        a = _np.ascontiguousarray(inputs[name])
        arrays[f"in_{name}"] = a
        args.append(nc.dram_tensor(f"in_{name}", a.shape, _mybir.dt.from_np(a.dtype), kind="ExternalInput").ap())
    args.append(nc.dram_tensor("out_0", (N_NODES, D), F32, kind="ExternalOutput").ap())
    build(nc, *args)
    r = _run(nc, [arrays], core_ids=[0])
    return r.results[0]["out_0"]
```

```python
import numpy as np
import concourse.bass as bass
from concourse import mybir
from contextlib import ExitStack

F32 = mybir.dt.float32
BF16 = mybir.dt.bfloat16
I32 = mybir.dt.int32
ALU = mybir.AluOpType
ACT = mybir.ActivationFunctionType
AXX = mybir.AxisListType.X

P = 128
N_NODES = 6250
D = 256
BLOCKS = -(-N_NODES // P)
NPAD = BLOCKS * P
TAIL = N_NODES - (BLOCKS - 1) * P
TRASH = NPAD - 1
NOWHERE = 1 << 20
HEADS = 4
OUT_A = 64
OUT_B = 4
EXPERTS = 4
HID = 512
U = 4
GROUP = U * P
NEG = -1.0e30
LN_EPS = 1e-5
RING = 4


class Graph:

    def __init__(self, name, edges, out, slope):
        self.name = name
        self.edges = edges
        self.cols = -(-edges // P)
        self.out = out
        self.row = HEADS * (out + 1)
        self.slope = slope
        groups = -(-self.cols * P // GROUP) + BLOCKS
        self.groups = -(-groups // RING) * RING
        self.list = self.cols * P


class Chain:

    def __init__(self, eng, sem):
        self.eng, self.sem, self.n, self.i, self.per = eng, sem, 0, None, 0

    def loop(self, i, per):
        self.i, self.per, self.start = i, per, self.n

    def end(self, trips):
        assert self.n - self.start == self.per, (self.n - self.start, self.per)
        self.n = self.start + self.per * trips
        self.i = None

    def mark(self, ins):
        ins.then_inc(self.sem, 1)
        self.n += 1

    def __call__(self, ins):
        self.mark(ins)
        self.wait()

    def wait(self, but=0):
        self.eng.wait_ge(self.sem, self.n - but if self.i is None else self.i * self.per + (self.n - but))


PIECE = 7
assert BLOCKS % PIECE == 0 and BLOCKS % 2 == 1


def by_pairs(eng, step):
    for b in range(3):
        step(b, b % 2, True)
    with eng.Fori(0, (BLOCKS - 5) // 2) as i:
        step(i * 2 + 3, 1, True)
        step(i * 2 + 4, 0, True)
    step(BLOCKS - 2, 1, False)
    step(BLOCKS - 1, 0, False)


def variance(link, V, stats, mean, sd, s_var):
    even, odd = 0, 3
    link.mark(V.tensor_tensor(mean[:, 0, :], stats[:, :, even + 1], stats[:, :, odd + 1], ALU.add))
    link.mark(V.tensor_tensor(mean[:, 1, :], stats[:, :, even + 1], stats[:, :, odd + 1], ALU.subtract))
    link(V.tensor_tensor(mean[:, 2, :], stats[:, :, even + 2], stats[:, :, odd + 2], ALU.add))
    link.mark(V.tensor_scalar(mean[:, 0, :], mean[:, 0, :], 0.5, None, ALU.mult))
    link(V.scalar_tensor_tensor(mean[:, 1, :], mean[:, 1, :], 0.25, mean[:, 1, :], ALU.mult, ALU.mult))
    link(V.scalar_tensor_tensor(mean[:, 1, :], mean[:, 2, :], 1.0 / D, mean[:, 1, :], ALU.mult, ALU.add))
    V.tensor_scalar(sd[:, 0, :], mean[:, 1, :], LN_EPS, None, ALU.add).then_inc(s_var, 1)


def build(nc, x, src, dst, gnn_W, gnn_a_src, gnn_a_dst, W_gat, att_src, att_dst, b_gat,
          ln_gamma, ln_beta, W1, b1, W2, b2, edge_index, out):
    A = Graph("a", src.shape[0], OUT_A, 0.01)
    B = Graph("b", edge_index.shape[1], OUT_B, 0.2)

    def dram(name, shape, dt):
        return nc.dram_tensor(name, shape, dt, kind="Internal").ap()

    for g in (A, B):
        g.table = dram(f"table_{g.name}", (NPAD, g.row), F32)
        g.ordered = dram(f"ordered_{g.name}", (g.list + GROUP, 2), I32)
        g.plan = dram(f"plan_{g.name}", (3, P * 4), I32)

    ctx = ExitStack()
    with ctx:
        def sb(name, shape, dt=F32, at=ctx):
            return at.enter_context(nc.sbuf_tensor(name, shape, dt))

        def sem(name):
            return ctx.enter_context(nc.semaphore(name))

        X = sb("X", [P, BLOCKS, D])
        ACC = sb("ACC", [P, BLOCKS, A.row])
        ident = sb("ident", [P, P])
        ident_neg = sb("ident_neg", [P, P], BF16)
        iota_row = sb("iota_row", [P, P])
        accB = sb("accB", [P, BLOCKS, B.row])
        for g in (A, B):
            g.ed = sb(f"ed_{g.name}", [P, BLOCKS, HEADS])
            g.mx = sb(f"mx_{g.name}", [P, BLOCKS, HEADS])
        B.pair = sb("pair_b", [P, B.cols, 2], I32)
        B.slot = sb("slot_b", [P, B.cols], I32)
        A.acc, B.acc = ACC, accB
        B.each = B.cols // (A.groups // RING) - 1
        B.early = B.cols - B.each * (A.groups // RING)

        index_and_nodes(nc, ctx, sb, sem, A, B, X, ident, ident_neg, iota_row,
                        x, src, dst, edge_index, gnn_W, gnn_a_src, gnn_a_dst)
        attend(nc, sem, A, ident, ident_neg, iota_row, B)
        nodes_b(nc, sem, A, B, X, ident, W_gat, att_src, att_dst)
        K, FC = HEADS * OUT_B, HID // P
        w1, w2 = sb("w1", [P, EXPERTS, 2, HID]), sb("w2", [P, EXPERTS, FC, D])
        b1c, b2b = sb("b1c", [P, EXPERTS, FC]), sb("b2b", [P, EXPERTS, D])
        vec = sb("vec", [P, 3, K])
        s_w = sem("expert_weights_loaded")

        def load_expert_weights(sp):
            for e in range(EXPERTS):
                sp.dma_start(w1[:, e], W1[e].rearrange("(k p) f -> p k f", p=P)).then_inc(s_w, 16)
                sp.dma_start(b1c[:, e, :], b1[e:e + 1, :].rearrange("u (c p) -> p (u c)", p=P), allow_slow_non_contiguous=True).then_inc(s_w, 16)
                sp.dma_start(w2[:, e], W2[e].rearrange("(c p) f -> p c f", p=P)).then_inc(s_w, 16)
            sp.dma_start(b2b[:].rearrange("p e f -> p (e f)"), b2.rearrange("(u e) f -> u (e f)", u=1).to_broadcast([P, EXPERTS * D])).then_inc(s_w, 16)
            for n, v in enumerate((b_gat, ln_gamma, ln_beta)):
                sp.dma_start(vec[:, n, :], v.rearrange("(u f) -> u f", u=1).to_broadcast([P, K])).then_inc(s_w, 16)

        attend(nc, sem, B, ident, ident_neg, iota_row, None, load_expert_weights)
        experts(nc, sem, A, B, X, w1, w2, b1c, b2b, vec, s_w, 16 * (3 * EXPERTS + 4), out)


def index_and_nodes(nc, ctx, sb, sem, A, B, X, ident, ident_neg, iota_row,
                    x, src, dst, edge_index, gnn_W, gnn_a_src, gnn_a_dst):
    ph = ExitStack()
    with ph:
        def tb(name, shape, dt=F32):
            return sb(name, shape, dt, ph)

        SC = 4
        T = A.cols
        BL2 = BLOCKS + BLOCKS % 2
        assert BL2 > BLOCKS
        assert max(A.groups, B.groups) + 2 <= 4 * P and B.cols <= T
        flat = A.acc[:, :, :].rearrange("p b f -> p (b f)")
        dst_a, src_a, next_a = [flat[:, k * T:(k + 1) * T].bitcast(I32) for k in range(3)]
        scan = [flat[:, k * T:(k + 1) * T] for k in (0, 1)]
        part = [flat[:, k * T:(k + 1) * T] for k in (2, 3)]
        pos = flat[:, 4 * T:5 * T]
        dst_b, src_b = tb("dst_b", [P, B.cols], I32), tb("src_b", [P, B.cols], I32)
        ones_t = tb("ones_t", [P, T], BF16)
        mask = tb("mask", [P, 2, T], BF16)
        signs = tb("signs", [P, 2, T], BF16)
        A.pair = tb("pair_a", [P, A.cols, 2], I32)
        A.slot = tb("slot_a", [P, A.cols], I32)
        for g in (A, B):
            g.hi = tb(f"hi_{g.name}", [P, g.cols], BF16)
            g.sign = tb(f"sign_{g.name}", [P, BL2])
            g.rowtot = tb(f"rowtot_{g.name}", [P, BLOCKS])
            g.start = tb(f"start_{g.name}", [P, BL2])
        grp = tb("grp", [P, 4])
        grp_i = tb("grp_i", [P, 3, 4], I32)
        grp_f = tb("grp_f", [P, 3, 4])
        past = tb("past", [P, 2, 4, BLOCKS])
        bad = tb("bad", [P, 1])
        unsorted = tb("unsorted", [P, 1], I32)
        bcol = tb("bcol", [P, BL2])
        edge_of = tb("edge_of", [P, BL2])
        ones_mat = tb("ones_mat", [P, P])
        lower = tb("lower", [P, P])
        small = tb("small", [P, 6, BLOCKS])
        small_i = tb("small_i", [P, BLOCKS], I32)
        tail = tb("tail", [P, U, 2], I32)
        stage = tb("stage", [P, 2, SC, 3], I32)
        wx = tb("wx_a", [P, 2, A.row + HEADS])
        a_bc = tb("a_bc", [P, 2, D])
        wprod = tb("wprod", [P, 2, 2, D])
        stats = tb("stats", [P, BLOCKS, 6])
        mean = tb("mean", [P, 3, BLOCKS])
        sd = tb("sd", [P, 2, BLOCKS])
        xn = tb("xn", [P, 2, D])
        xt = tb("xt", [P, 2, 2, P])
        ps_cnt = ph.enter_context(nc.psum_tensor("ps_cnt", [P, 512], F32))
        ps_t = ph.enter_context(nc.psum_tensor("ps_t", [P, 2, 4, P], F32))
        ps_z = ph.enter_context(nc.psum_tensor("ps_z", [P, 2, 512], F32))

        s_const = sem("i_const")
        s_idx = sem("i_edges_loaded")
        s_idxb = sem("i_edges_b_loaded")
        s_x = sem("i_x_loaded")
        s_w = sem("i_w_loaded")
        s_fill = sem("i_tails_stored")
        s_fillm = sem("i_tail_made")
        s_plan, s_plans = sem("i_plan_made"), sem("i_plan_stored")
        s_flag, s_list = sem("i_order_known"), sem("i_list_copied")
        s_hi, s_cnt = sem("i_blocks_known"), sem("i_counted")
        s_tot = sem("i_row_totals")
        s_pre = sem("i_prefixes")
        s_part, s_sum = sem("i_part_made"), sem("i_part_added")
        s_rec, s_reca = sem("i_places_b"), sem("i_places_a")
        s_st = sem("i_staged")
        s_sc = [sem(f"i_scattered{h}") for h in range(2)]
        s_see, s_seea = sem("i_pool_saw"), sem("i_act_saw")
        s_dve = sem("i_dve_chain")
        s_zero = sem("i_cleared")
        s_var = sem("i_var")
        s_sd = sem("i_sd")
        s_xn = sem("i_xn")
        s_xtp = sem("i_xt_psum")
        s_xt = sem("i_xt")
        s_z = sem("i_z")
        s_zc = sem("i_z_copied")
        s_tab = sem("i_table_stored")
        s_pair = sem("i_pairs_made")

        with nc.Block() as block:
            @block.gpsimd
            def _(pool):
                nc.gpsimd.iota(edge_of[:], pattern=[[-1, BL2]], base=0, channel_multiplier=0,
                               allow_small_or_imprecise_dtypes=True).then_inc(s_const, 1)
                nc.gpsimd.iota(bcol[:], pattern=[[1, BL2]], base=0, channel_multiplier=0,
                               allow_small_or_imprecise_dtypes=True).then_inc(s_const, 1)
                nc.gpsimd.memset(tail[:, :, 0:1], 0).then_inc(s_fillm, 1)
                nc.gpsimd.memset(tail[:, :, 1:2], NOWHERE).then_inc(s_fillm, 1)
                nc.gpsimd.memset(ident[:], 0.0).then_inc(s_const, 1)
                nc.gpsimd.memset(lower[:], 1.0).then_inc(s_const, 1)
                nc.gpsimd.memset(ones_mat[:], 1.0).then_inc(s_const, 1)
                pool.wait_ge(s_const, 5)
                nc.gpsimd.affine_select(out=ident[:], in_=ident[:], compare_op=ALU.not_equal, fill=1.0,
                                        base=0, pattern=[[-1, P]], channel_multiplier=1).then_inc(s_const, 1)
                nc.gpsimd.affine_select(out=lower[:], in_=lower[:], compare_op=ALU.is_gt, fill=0.0,
                                        base=0, pattern=[[1, P]], channel_multiplier=-1).then_inc(s_const, 1)
                nc.gpsimd.iota(iota_row[:], pattern=[[1, P]], base=0, channel_multiplier=0,
                               allow_small_or_imprecise_dtypes=True).then_inc(s_const, 1)
                nc.gpsimd.iota(grp[:], pattern=[[1, 4]], base=0, channel_multiplier=4,
                               allow_small_or_imprecise_dtypes=True).then_inc(s_const, 1)
                pool.wait_ge(s_const, 9)

                def add_parts(g, before):
                    with pool.Fori(0, BL2 // 2) as i:
                        for h in range(2):
                            pool.wait_ge(s_part, i * 2 + (before + h + 1))
                            pool.sem_inc(s_see, 1)
                            pool.wait_ge(s_sum, i * 2 + (before + h))
                            pool.sem_inc(s_see, 1)
                            nc.gpsimd.tensor_tensor(pos[:, 0:g.cols], pos[:, 0:g.cols], part[h][:, 0:g.cols], ALU.add).then_inc(s_sum, 1)

                def scatter_columns(g, n, before):
                    def scatter(i, h):
                        at = i * (2 * SC) + h * SC
                        cols = slice(at, at + SC) if isinstance(i, int) else bass.ds(at, SC)
                        nc.gpsimd.tensor_copy(stage[:, h, :, 0], g.slot[:, cols]).then_inc(s_st, 1)
                        nc.gpsimd.tensor_copy(stage[:, h, :, 1:3], g.pair[:, cols, :]).then_inc(s_st, 1)
                        pool.wait_ge(s_st, i * 4 + (before * 4 + 2 * h + 2))
                        pool.sem_inc(s_see, 1)
                        for c in range(SC):
                            pool.indirect_dma_start(
                                out=g.ordered[:, :],
                                out_offset=bass.IndirectOffsetOnAxis(ap=stage[:, h, c, 0:1], axis=0),
                                in_=stage[:, h, c, 1:3], in_offset=None).then_inc(s_sc[h], 16)

                    turns = n // (2 * SC)
                    for h in range(2):
                        scatter(0, h)
                    with pool.Fori(1, turns) as i:
                        for h in range(2):
                            pool.wait_ge(s_sc[h], i * (16 * SC) + before * (16 * SC))
                            pool.sem_inc(s_see, 1)
                            scatter(i, h)
                    if n > turns * 2 * SC:
                        assert n == turns * 2 * SC + SC
                        pool.wait_ge(s_sc[0], (before + turns) * 16 * SC)
                        scatter(turns, 0)
                    for h in range(2):
                        pool.wait_ge(s_sc[h], 16 * SC * (before + -(-(n // SC - h) // 2)))

                pool.sem_inc(s_sum, 2)
                add_parts(B, 2)
                pool.wait_ge(s_rec, 1)
                scatter_columns(B, B.early, 0)
                pool.wait_ge(s_flag, 1)
                out_of_order = pool.value_load(unsorted[0:1, 0:1], min_val=0, max_val=A.list)
                with pool.If(out_of_order != 0):
                    add_parts(A, 2 + BL2)
                    pool.wait_ge(s_reca, 1)
                    pool.wait_ge(s_list, 16)
                    scatter_columns(A, A.cols, B.early // (2 * SC))

            full = A.edges // A.cols
            rest = A.edges - full * A.cols
            assert full < P and rest > 1

            @block.sync
            def _(sp):
                for n, t in enumerate((src_b, dst_b)):
                    sp.dma_start(t[:], edge_index[n, :].rearrange("(p t) -> p t", t=B.cols)).then_inc(s_idxb, 16)
                sp.wait_ge(s_zero, 1)
                for tile, first in ((dst_a, 0), (next_a, 1)):
                    sp.dma_start(tile[0:full, :], dst[first:first + full * A.cols].rearrange("(p t) -> p t", t=A.cols)).then_inc(s_idx, 16)
                    sp.dma_start(tile[full:full + 1, 0:rest - first],
                                 dst[first + full * A.cols:A.edges].rearrange("(p t) -> p t", p=1)).then_inc(s_idx, 16)
                sp.dma_start(src_a[0:full, :], src[0:full * A.cols].rearrange("(p t) -> p t", t=A.cols)).then_inc(s_idx, 16)
                sp.dma_start(src_a[full:full + 1, 0:rest], src[full * A.cols:A.edges].rearrange("(p t) -> p t", p=1)).then_inc(s_idx, 16)
                sp.wait_ge(s_zero, 2)
                sp.dma_start(X[:, 0:BLOCKS - 1, :], x[0:(BLOCKS - 1) * P, :].rearrange("(b p) f -> p b f", p=P)).then_inc(s_x, 16)
                sp.dma_start(X[0:TAIL, BLOCKS - 1, :], x[(BLOCKS - 1) * P:N_NODES, :]).then_inc(s_x, 16)
                for k in range(2):
                    sp.dma_start(wx[:, k, 0:A.row].rearrange("p (h o) -> p h o", h=HEADS)[:, :, 0:OUT_A],
                                 gnn_W[:, k * P:(k + 1) * P, :].rearrange("h p o -> p h o")).then_inc(s_w, 16)
                for n, a in enumerate((gnn_a_src, gnn_a_dst)):
                    sp.dma_start(a_bc[:, n, :], a.rearrange("(u h) o -> u (h o)", u=1).to_broadcast([P, D])).then_inc(s_w, 16)
                sp.wait_ge(s_fillm, 2)
                for g in (A, B):
                    sp.dma_start(g.ordered[g.list:g.list + GROUP, :].rearrange("(p t) c -> p (t c)", p=P),
                                 tail[:].rearrange("p t c -> p (t c)")).then_inc(s_fill, 16)
                sp.wait_ge(s_pair, 1)
                sp.dma_start(A.ordered[0:A.list, :].rearrange("(p t) c -> p (t c)", p=P),
                             A.pair[:].rearrange("p t c -> p (t c)")).then_inc(s_list, 16)
                for n, g in enumerate((B, A)):
                    sp.wait_ge(s_plan, n + 1)
                    sp.dma_start(g.plan.rearrange("k (p c) -> p k c", p=P), grp_i[:]).then_inc(s_plans, 16)
                    sp.wait_ge(s_plans, 16 * (n + 1))
                for c in range(0, BLOCKS, PIECE):
                    sp.wait_ge(s_zc, c + PIECE)
                    sp.dma_start(A.table[c * P:(c + PIECE) * P, :].rearrange("(b p) f -> p b f", p=P),
                                 A.acc[:, c:c + PIECE, :]).then_inc(s_tab, 16)
                sp.wait_ge(s_tab, 16 * (BLOCKS // PIECE))
                sp.wait_ge(s_list, 16)
                sp.wait_ge(s_fill, 32)

            @block.vector
            def _(dve):
                link = Chain(dve, s_dve)
                V = nc.vector
                V.memset(dst_a, TRASH)
                V.memset(next_a, TRASH)
                V.memset(src_a, 0).then_inc(s_zero, 1)
                V.memset(X[:, BLOCKS - 1, :], 0.0).then_inc(s_zero, 1)
                V.memset(ones_t[:], 1.0)
                dve.wait_ge(s_const, 2)
                link(V.tensor_scalar(edge_of[:], edge_of[:], 0.5, None, ALU.add))
                for g in (A, B):
                    V.memset(g.mx[:], NEG)
                    link(V.memset(g.start[:], 0.0))

                def blocks_of(g, src_i, dst_i):
                    V.tensor_scalar(g.pair[:, :, 0], src_i, N_NODES - 1, None, ALU.min)
                    link(V.tensor_scalar(g.pair[:, :, 1], dst_i, TRASH, None, ALU.min))
                    link(V.tensor_scalar(dst_i, g.pair[:, :, 1], 7, None, ALU.logical_shift_right))
                    V.tensor_copy(g.hi[:], dst_i).then_inc(s_hi, 1)

                dve.wait_ge(s_idxb, 32)
                blocks_of(B, src_b[:], dst_b[:])
                dve.wait_ge(s_idx, 96)
                blocks_of(A, src_a, dst_a)
                dve.sem_inc(s_pair, 1)
                link(V.tensor_scalar(next_a, next_a, TRASH, None, ALU.min))
                link(V.tensor_tensor(pos, next_a, A.pair[:, :, 1], ALU.is_lt))
                link(V.tensor_reduce(bad[:], pos, AXX, ALU.add))

                dve.wait_ge(s_x, 32)
                with dve.Fori(0, BLOCKS // PIECE) as c:
                    link.loop(c, PIECE)
                    for b in range(PIECE):
                        one = bass.ds(c * PIECE + b, 1)
                        link.mark(V.bn_stats(stats[:, one, :].rearrange("p b f -> p (b f)"),
                                             X[:, one, :].rearrange("p b f -> p (b f)")))
                    link.end(BLOCKS // PIECE)
                link.wait()
                variance(link, V, stats, mean, sd, s_var)

                dve.wait_ge(s_w, 64)
                for k in range(2):
                    w_ho = wx[:, k, 0:A.row].rearrange("p (h o) -> p h o", h=HEADS)
                    for n in range(2):
                        V.tensor_tensor(wprod[:, k, n, :].rearrange("p (h o) -> p h o", h=HEADS), w_ho[:, :, 0:OUT_A],
                                        a_bc[:, n, :].rearrange("p (h o) -> p h o", h=HEADS), ALU.mult).then_inc(s_dve, 1)
                        link.n += 1
                link.wait()
                for k in range(2):
                    w_ho = wx[:, k, 0:A.row].rearrange("p (h o) -> p h o", h=HEADS)
                    for n in range(2):
                        score = w_ho[:, :, OUT_A] if n == 0 else wx[:, k, A.row:]
                        link.mark(V.tensor_reduce(score, wprod[:, k, n, :].rearrange("p (h o) -> p h o", h=HEADS), AXX, ALU.add))
                link.wait()

                def plan(g, n):
                    dve.wait_ge(s_cnt, 2 + BL2 * (n + 1))
                    link(V.tensor_tensor(g.rowtot[:], g.sign[:, 0:BLOCKS], g.sign[:, 1:BLOCKS + 1], ALU.subtract))
                    V.tensor_scalar(g.rowtot[:], g.rowtot[:], 0.5, None, ALU.mult).then_inc(s_tot, 1)
                    dve.wait_ge(s_pre, n + 1)
                    count, ends_, gcount, gend, gpast, off = [small[:, k, :] for k in range(6)]
                    link(V.tensor_scalar(small_i[:], ps_cnt[:, 0:BLOCKS], float(GROUP - 1), None, ALU.add))
                    link(V.tensor_scalar(small_i[:], small_i[:], GROUP.bit_length() - 1, None, ALU.logical_shift_right))
                    link.mark(V.tensor_copy(gcount, small_i[:]))
                    link(V.tensor_copy(count, ps_cnt[:, 0:BLOCKS]))
                    link.mark(V.tensor_tensor_scan(gend, ones_t[:, 0:BLOCKS], gcount, 0.0, ALU.mult, ALU.add))
                    link(V.tensor_tensor_scan(ends_, ones_t[:, 0:BLOCKS], count, 0.0, ALU.mult, ALU.add))
                    link(V.tensor_tensor(off, ends_, count, ALU.subtract))
                    link.mark(V.scalar_tensor_tensor(g.start[:, 0:BLOCKS], off, 1.0, ps_cnt[:, 64:64 + BLOCKS], ALU.subtract, ALU.add))
                    link(V.tensor_tensor(gpast, gend, gcount, ALU.subtract))
                    link(V.scalar_tensor_tensor(off, gpast, -float(GROUP), off, ALU.mult, ALU.add))
                    link(V.memset(gpast, 0.0))
                    link.mark(V.tensor_tensor(gpast[:, 0:BLOCKS - 1], off[:, 1:BLOCKS], off[:, 0:BLOCKS - 1], ALU.subtract))
                    link(V.tensor_tensor(past[:, 0], grp[:].unsqueeze(2).to_broadcast([P, 4, BLOCKS]),
                                         gend.unsqueeze(1).to_broadcast([P, 4, BLOCKS]), ALU.is_ge))
                    link.mark(V.tensor_tensor(past[:, 1], past[:, 0], gpast.unsqueeze(1).to_broadcast([P, 4, BLOCKS]), ALU.mult))
                    link(V.tensor_reduce(grp_f[:, 0, :], past[:, 0], AXX, ALU.add))
                    link.mark(V.tensor_reduce(grp_f[:, 1, :], past[:, 1], AXX, ALU.add))
                    link(V.tensor_scalar(grp_f[:, 0, :], grp_f[:, 0, :], float(BLOCKS - 1), None, ALU.min))
                    link(V.scalar_tensor_tensor(grp_f[:, 2, :], grp[:], float(GROUP), grp_f[:, 1, :], ALU.mult, ALU.add))
                    if n:
                        dve.wait_ge(s_plans, 16)
                    link.mark(V.tensor_scalar(grp_i[:, 2, :].bitcast(F32), grp_f[:, 0, :], float(P), None, ALU.mult))
                    link(V.tensor_copy(grp_i[:, 0, :], grp_f[:, 0, :]))
                    V.tensor_scalar(grp_i[:, 1, :], grp_f[:, 2, :], float(g.list), None, ALU.min).then_inc(s_plan, 1)

                def places(g, before):
                    T = g.cols
                    link(V.memset(pos[:, 0:T], 0.0))
                    with dve.Fori(0, BL2 // 2) as i:
                        link.loop(i, 4)
                        for h in range(2):
                            link.mark(V.tensor_scalar(mask[:, h, 0:T], g.hi[:], bcol[:, bass.ds(i * 2 + h, 1)], None, ALU.is_equal))
                        dve.wait_ge(s_part, i * 2 + before)
                        for h in range(2):
                            link.wait(1)
                            link.mark(V.tensor_tensor_scan(scan[h][:, 0:T], ones_t[:, 0:T], mask[:, h, 0:T],
                                                           g.start[:, bass.ds(i * 2 + h, 1)], ALU.mult, ALU.add))
                        for h in range(2):
                            link.wait(1 - h)
                            dve.wait_ge(s_sum, i * 2 + (before - 1 + h))
                            V.scalar_tensor_tensor(part[h][:, 0:T], g.hi[:], bcol[:, bass.ds(i * 2 + h, 1)], scan[h][:, 0:T],
                                                   ALU.is_equal, ALU.mult).then_inc(s_part, 1)
                        link.end(BL2 // 2)
                    dve.wait_ge(s_sum, BL2 + before)
                    link(V.tensor_copy(g.slot[:], pos[:, 0:T]))

                plan(B, 0)
                dve.sem_inc(s_part, 2)
                places(B, 2)
                dve.sem_inc(s_rec, 1)
                dve.wait_ge(s_const, 9)
                V.tensor_scalar(ident_neg[:], ident[:], NEG, None, ALU.mult)
                plan(A, 1)
                V.tensor_scalar(unsorted[:], ps_cnt[:, 128:129], 1.0, None, ALU.mult).then_inc(s_flag, 1)
                dve.wait_ge(s_flag, 1)
                out_of_order = dve.value_load(unsorted[0:1, 0:1], min_val=0, max_val=A.list)
                before = link.n
                with dve.If(out_of_order != 0):
                    places(A, 2 + BL2)
                    dve.sem_inc(s_reca, 1)
                with dve.Else():
                    dve.sem_inc(s_dve, link.n - before)

                dve.wait_ge(s_sd, 1)
                link(V.reciprocal(sd[:, 1, :], sd[:, 1, :]))

                def norm(b, v):
                    one = slice(b, b + 1) if isinstance(b, int) else bass.ds(b, 1)
                    if not isinstance(b, int) or b >= 2:
                        dve.wait_ge(s_xtp, b - 1)
                    V.tensor_scalar(xn[:, v, :], X[:, one, :].rearrange("p b f -> p (b f)"),
                                    mean[:, 0, one], sd[:, 1, one],
                                    ALU.subtract, ALU.mult).then_inc(s_xn, 1)

                def step(b, v, more):
                    if more:
                        norm(b + 2, v)
                    one = slice(b, b + 1) if isinstance(b, int) else bass.ds(b, 1)
                    dve.wait_ge(s_z, b + 1)
                    V.tensor_scalar(A.acc[:, one, :].rearrange("p b f -> p (b f)"), ps_z[:, v, 0:A.row], 1.0, None, ALU.mult)
                    V.tensor_scalar(A.ed[:, one, :].rearrange("p b h -> p (b h)"), ps_z[:, v, A.row:A.row + HEADS],
                                    1.0, None, ALU.mult).then_inc(s_zc, 1)

                norm(0, 0)
                norm(1, 1)
                by_pairs(dve, step)

            @block.scalar
            def _(act):
                act.wait_ge(s_dve, 1)
                nc.scalar.activation(signs[:, 0, 0:1], edge_of[:, 0:1], ACT.Sign).then_inc(s_cnt, 2)
                for n, g in enumerate((B, A)):
                    act.wait_ge(s_hi, n + 1)
                    with act.Fori(0, BL2 // 2) as i:
                        for h in range(2):
                            act.wait_ge(s_cnt, i * 2 + (n * BL2 + h + 1))
                            act.sem_inc(s_seea, 1)
                            nc.scalar.activation(signs[:, h, 0:g.cols], g.hi[:], ACT.Sign, bias=edge_of[:, bass.ds(i * 2 + h, 1)],
                                                 accum_out=g.sign[:, bass.ds(i * 2 + h, 1)]).then_inc(s_cnt, 1)
                act.wait_ge(s_var, 1)
                nc.scalar.activation(sd[:, 1, :], sd[:, 0, :], ACT.Sqrt).then_inc(s_sd, 1)

                def step(b, v, more):
                    act.wait_ge(s_xtp, b + 1)
                    if not isinstance(b, int) or b >= 2:
                        act.wait_ge(s_z, b - 1)
                    nc.scalar.activation(xt[:, v], ps_t[:, v, 0:2], ACT.Copy).then_inc(s_xt, 1)

                by_pairs(act, step)

            @block.tensor
            def _(pe):
                pe.wait_ge(s_const, 9)
                for n, g in enumerate((B, A)):
                    pe.wait_ge(s_tot, n + 1)
                    nc.tensor.matmul(ps_cnt[:, 0:BLOCKS], ones_mat[:], g.rowtot[:], start=True, stop=True)
                    nc.tensor.matmul(ps_cnt[:, 128:129], ones_mat[:], bad[:], start=True, stop=True)
                    nc.tensor.matmul(ps_cnt[:, 64:64 + BLOCKS], lower[:], g.rowtot[:], start=True, stop=True).then_inc(s_pre, 1)

                def turn_rows(b, v):
                    pe.wait_ge(s_xn, b + 1)
                    if not isinstance(b, int) or b >= 2:
                        pe.wait_ge(s_xt, b - 1)
                    for k in range(2):
                        last = nc.tensor.transpose(ps_t[:, v, k, :], xn[:, v, k * P:(k + 1) * P], ident[:])
                    last.then_inc(s_xtp, 1)

                def step(b, v, more):
                    pe.wait_ge(s_xt, b + 1)
                    if not isinstance(b, int) or b >= 2:
                        pe.wait_ge(s_zc, b - 1)
                    for k in range(2):
                        last = nc.tensor.matmul(ps_z[:, v, 0:A.row + HEADS], xt[:, v, k, :], wx[:, k, :], start=(k == 0), stop=(k == 1))
                    last.then_inc(s_z, 1)
                    if more:
                        turn_rows(b + 2, v)

                turn_rows(0, 0)
                turn_rows(1, 1)
                by_pairs(pe, step)


def attend(nc, sem, g, ident, ident_neg, iota_row, later, preload=None):
    ph = ExitStack()
    n_ = g.name
    G = g.groups
    with ph:
        def tb(name, shape, dt=F32):
            return ph.enter_context(nc.sbuf_tensor(name + "_" + n_, shape, dt))

        def pt(name, shape):
            return ph.enter_context(nc.psum_tensor(name + "_" + n_, shape, F32))

        o1 = g.out + 1
        dve_tiles = U - 1 if g.out > 16 else U
        blk = tb("blk", [1, 4 * P], I32)
        first = tb("first", [1, 4 * P], I32)
        base = tb("base", [P, 4 * P])
        pair = tb("pair_now", [P, RING, U, 2], I32)
        if later:
            SC = later.each
            stage = tb("stage_sc", [P, SC, 3], I32)
        rows = tb("rows", [P, RING, U * HEADS, o1])
        msg = tb("msg", [P, 2, U * HEADS, o1])
        dl_neg = tb("dl_neg", [P, U])
        away = tb("away", [P, U, P], BF16)
        onehot = tb("onehot", [P, RING, U, P])
        other = tb("other", [P, 2, U, P], BF16)
        onehot_t = tb("onehot_t", [P, 2, U, P])
        tmax4 = tb("tmax4", [P, U, HEADS])
        tmax = tb("tmax", [P, 4, HEADS])
        node = tb("node", [P, 2, 2 * HEADS])
        drop = tb("drop", [P, RING, HEADS])
        scale = tb("scale", [P, RING, HEADS])
        u = tb("u", [P, 4, U * HEADS])
        ps_es = pt("ps_es", [P, U, HEADS, P])
        ps_ot = pt("ps_ot", [P, U, P])
        ps_ge = pt("ps_ge", [P, 2, U, 2 * HEADS])
        ps_out = pt("ps_out", [P, 2, 512])

        def sm(name):
            return sem(name + "_" + n_)

        s_plan, s_see = sm("plan_loaded"), sm("pool_saw")
        s_sees, s_seea = sm("sync_saw"), sm("act_saw")
        s_pair = [sm(f"pairs_loaded{q}") for q in range(RING)]
        s_st, s_sc = sm("scatter_staged"), sm("scattered")
        s_rows = [sm(f"rows_gathered{q}") for q in range(RING)]
        s_neg, s_away = sm("dl_negated"), sm("away_ready")
        s_oh, s_oth = sm("onehot_ready"), sm("other_ready")
        s_otp, s_ot = sm("onehot_t_psum"), sm("onehot_t_ready")
        s_es, s_mx = sm("scores_spread"), sm("scores_maxed")
        s_drop, s_node, s_scale = sm("drop_ready"), sm("node_ready"), sm("scale_ready")
        s_ge, s_u, s_ex, s_msg = sm("edge_values"), sm("exponent_ready"), sm("weight_ready"), sm("msg_ready")
        s_out, s_acc = sm("sums_ready"), sm("sums_added")
        s_msga = sm("msg_by_act_ready")
        s_dve = sm("dve_chain")
        trips = G // RING - 1

        assert trips % 2 == 0

        def by_groups(eng, step, link=None, marks=0):
            for q in range(RING):
                step(0, q, q, q >= 2)
            with eng.Fori(0, trips // 2) as i:
                if link:
                    link.loop(i, 2 * RING * marks)
                for v in range(2 * RING):
                    step(i * 2 + (1 + v // RING), i * (2 * RING) + (RING + v), v % RING, v >= 2)
                if link:
                    link.end(trips // 2)

        with nc.Block() as block:
            @block.sync
            def _(sp):
                sp.dma_start(blk[:], g.plan[0:1, :]).then_inc(s_plan, 16)
                sp.dma_start(first[:], g.plan[1:2, :]).then_inc(s_plan, 16)
                sp.dma_start(base[:].bitcast(I32), g.plan[2:3, :].to_broadcast([P, 4 * P])).then_inc(s_plan, 16)
                sp.wait_ge(s_plan, 48)

                def load(grp, q):
                    c = slice(grp, grp + 1) if isinstance(grp, int) else bass.ds(grp, 1)
                    e = sp.value_load(first[0:1, c], min_val=0, max_val=g.list)
                    sp.dma_start(pair[:, q].rearrange("p j c -> p (j c)"),
                                 g.ordered[bass.ds(e, GROUP), :].rearrange("(p j) c -> p (j c)", p=P)).then_inc(s_pair[q], 16)

                for q in range(RING):
                    load(q, q)

                def reload(i, q):
                    sp.wait_ge(s_rows[q], (i + 1) * (16 * U))
                    sp.sem_inc(s_sees, 1)
                    sp.wait_ge(s_neg, i * RING + (q + 1))
                    sp.sem_inc(s_sees, 1)
                    load(i * RING + (RING + q), q)

                with sp.Fori(0, trips) as i:
                    for q in range(RING):
                        reload(i, q)
                for q in range(2):
                    reload(trips, q)
                if preload:
                    preload(sp)

            @block.gpsimd
            def _(pool):
                pool.wait_ge(s_plan, 48)

                def gather(i, q):
                    pool.wait_ge(s_pair[q], i * 16 + 16)
                    if not isinstance(i, int):
                        pool.wait_ge(s_msg, i * RING + (q + 1 - RING))
                        if dve_tiles < U:
                            pool.wait_ge(s_msga, i * RING + (q + 1 - RING))
                    pool.sem_inc(s_see, 1)
                    for j in range(U):
                        pool.indirect_dma_start(
                            out=rows[:, q, j * HEADS:(j + 1) * HEADS, :].rearrange("p h o -> p (h o)"), out_offset=None,
                            in_=g.table[:, :],
                            in_offset=bass.IndirectOffsetOnAxis(ap=pair[:, q, j, 0:1], axis=0)).then_inc(s_rows[q], 16)

                def stage_columns(turn):
                    if not isinstance(turn, int) or turn:
                        pool.wait_ge(s_sc, turn * (16 * SC))
                        pool.sem_inc(s_see, 1)
                    at = turn * SC + later.early
                    c = slice(at, at + SC) if isinstance(turn, int) else bass.ds(at, SC)
                    nc.gpsimd.tensor_copy(stage[:, :, 0], later.slot[:, c]).then_inc(s_st, 1)
                    nc.gpsimd.tensor_copy(stage[:, :, 1:3], later.pair[:, c, :]).then_inc(s_st, 1)
                    pool.wait_ge(s_st, turn * 2 + 2)
                    pool.sem_inc(s_see, 1)

                def scatter(c):
                    pool.indirect_dma_start(
                        out=later.ordered[:, :],
                        out_offset=bass.IndirectOffsetOnAxis(ap=stage[:, c, 0:1], axis=0),
                        in_=stage[:, c, 1:3], in_offset=None).then_inc(s_sc, 16)

                def turn(i):
                    if later:
                        stage_columns(i)
                    for q in range(RING):
                        gather(i, q)
                        if later:
                            for c in range(q * SC // (RING - 1), min(SC, (q + 1) * SC // (RING - 1))):
                                scatter(c)

                turn(0)
                with pool.Fori(0, trips // 2) as i:
                    for k in range(2):
                        turn(i * 2 + (k + 1))
                if later:
                    pool.wait_ge(s_sc, 16 * (later.cols - later.early))

            @block.vector
            def _(dve):
                link = Chain(dve, s_dve)
                dve.wait_ge(s_plan, 48)
                if g.name == "a":
                    nc.vector.memset(g.acc[:, :, :], 0.0)

                def block_of(grp):
                    c = bass.ds(grp, 1) if not isinstance(grp, int) else slice(grp, grp + 1)
                    return dve.value_load(blk[0:1, c], min_val=0, max_val=BLOCKS - 1)

                blocks = [None] * RING

                def at(t, b):
                    return t[:, bass.ds(b, 1), :].rearrange("p b f -> p (b f)")

                def step(turn, it, q, near, now=True):
                    static = isinstance(it, int)
                    prev, prev2 = not static or 1 <= it <= G, not static or it >= 2
                    p, r = (q - 1) % 2, (q - 1) % RING
                    p2, r2 = q % 2, (q - 2) % RING
                    new = node[:, q % 2, :]
                    u4 = [u[:, n, :].rearrange("p (j h) -> p j h", j=U) for n in range(3)]

                    def source_max(j):
                        if now:
                            dve.wait_ge(s_es, it * U + (j + 1))
                            nc.vector.tensor_reduce(tmax4[:, j, :], ps_es[:, j], AXX, ALU.max).then_inc(s_mx, 1)

                    def exponent(k):
                        if not prev:
                            return
                        if k == 0:
                            dve.wait_ge(s_ge, it)
                            link.mark(nc.vector.tensor_tensor(u4[0], ps_ge[:, p, :, 0:HEADS],
                                                              rows[:, r, :, g.out].rearrange("p (j h) -> p j h", j=U), ALU.add))
                            return
                        link.wait(1 if k == 3 and now else 0)
                        if k == 1:
                            link.mark(nc.vector.scalar_tensor_tensor(u[:, 1, :], u[:, 0, :], g.slope, u[:, 0, :], ALU.mult, ALU.max))
                        if k == 2:
                            link.mark(nc.vector.tensor_tensor(u4[2], u4[1], ps_ge[:, p, :, HEADS:], ALU.subtract))
                        if k == 3:
                            nc.vector.tensor_scalar(u[:, 3, :], u[:, 2, :], 0.0, None, ALU.min).then_inc(s_u, 1)

                    source_max(0)
                    source_max(1)
                    if now:
                        b = blocks[q] = block_of(it)
                    exponent(0)
                    source_max(2)
                    exponent(1)
                    if prev2:
                        b2 = blocks[q - 2] if near else block_of(it - 2)
                    source_max(3)
                    exponent(2)
                    if now:
                        dve.wait_ge(s_mx, it * U + U)
                        link.mark(nc.vector.tensor_reduce(tmax[:, 0, :], tmax4[:].rearrange("p j h -> p h j"), AXX, ALU.max))
                    exponent(3)
                    if prev2:
                        a = g.acc[:, bass.ds(b2, 1), :].rearrange("p b (h o) -> p (b h) o", h=HEADS)
                        dve.wait_ge(s_scale, it - 1)
                        if not static or it >= 3:
                            dve.wait_ge(s_acc, it - 2)
                        link.mark(nc.vector.tensor_tensor(a, a, scale[:, r2, :].unsqueeze(2).to_broadcast([P, HEADS, o1]), ALU.mult))
                    if now:
                        link.wait(1 if prev2 else 0)
                        link.mark(nc.vector.tensor_tensor(tmax[:, 1, :], tmax[:, 0, :], at(g.ed, b), ALU.add))
                        link.wait()
                        link.mark(nc.vector.scalar_tensor_tensor(tmax[:, 2, :], tmax[:, 1, :], g.slope, tmax[:, 1, :], ALU.mult, ALU.max))
                    link.wait()
                    if now:
                        link(nc.vector.tensor_tensor(new[:, HEADS:], tmax[:, 2, :], at(g.mx, b), ALU.max))
                        nc.vector.tensor_tensor(drop[:, q, :], at(g.mx, b), new[:, HEADS:], ALU.subtract).then_inc(s_drop, 1)
                        nc.vector.tensor_scalar(new[:, 0:HEADS], at(g.ed, b), 1.0, None, ALU.mult).then_inc(s_node, 1)
                    if prev:
                        dve.wait_ge(s_ex, it)
                        mine = slice(0, dve_tiles * HEADS)
                        nc.vector.tensor_tensor(msg[:, p, mine, 0:g.out], rows[:, r, mine, 0:g.out],
                                                msg[:, p, mine, g.out:].to_broadcast([P, dve_tiles * HEADS, g.out]),
                                                ALU.mult).then_inc(s_msg, 1)
                    if prev2:
                        dve.wait_ge(s_out, it - 1)
                        nc.vector.tensor_tensor(a, a, ps_out[:, p2, 0:g.row].rearrange("p (h o) -> p h o", h=HEADS), ALU.add).then_inc(s_acc, 1)
                    if now:
                        dve.wait_ge(s_drop, it + 1)
                        link.mark(nc.vector.tensor_scalar(at(g.mx, b), new[:, HEADS:], 1.0, None, ALU.mult))

                by_groups(dve, step, link, 9)
                for k in range(2):
                    step(None, G + k, k, False, now=False)

            @block.scalar
            def _(act):
                act.wait_ge(s_plan, 48)

                def make_onehot(i, it, q):
                    static = isinstance(it, int)
                    act.wait_ge(s_pair[q], i * 16 + 16)
                    act.sem_inc(s_seea, 1)
                    nc.scalar.activation(dl_neg[:], pair[:, q, :, 1], ACT.Identity, scale=-1.0,
                                         bias=base[:, slice(it, it + 1) if static else bass.ds(it, 1)]).then_inc(s_neg, 1)
                    act.wait_ge(s_neg, it + 1)
                    for j in range(U):
                        last = nc.scalar.activation(away[:, j, :], iota_row[:], ACT.Abs, bias=dl_neg[:, j:j + 1])
                    last.then_inc(s_away, 1)
                    act.wait_ge(s_away, it + 1)
                    if not static or it >= RING:
                        act.wait_ge(s_out, it - (RING - 1))
                    nc.scalar.activation(onehot[:, q], away[:], ACT.Relu, bias=1.0, scale=-1.0).then_inc(s_oh, 1)
                    act.wait_ge(s_oh, it + 1)
                    if not static or it >= 2:
                        act.wait_ge(s_es, it * U - U)
                    nc.scalar.activation(other[:, q % 2], onehot[:, q], ACT.Identity, bias=1.0, scale=-1.0).then_inc(s_oth, 1)

                def copy_transposed(it, q):
                    act.wait_ge(s_otp, it + 1)
                    if not isinstance(it, int) or it >= 2:
                        act.wait_ge(s_ge, it - 1)
                    nc.scalar.activation(onehot_t[:, q % 2], ps_ot[:], ACT.Copy).then_inc(s_ot, 1)

                def step(turn, it, q, near, now=True):
                    static = isinstance(it, int)
                    prev = not static or it >= 1
                    if now:
                        make_onehot(turn + (q + 2) // RING, it + 2, (q + 2) % RING)
                        copy_transposed(it + 1, q + 1)
                    if prev:
                        act.wait_ge(s_u, it)
                        if not static or it >= 3:
                            act.wait_ge(s_out, it - 2)
                        p, r = (q - 1) % 2, (q - 1) % RING
                        nc.scalar.activation(msg[:, p, :, g.out], u[:, 3, :], ACT.Exp).then_inc(s_ex, 1)
                        act.wait_ge(s_ex, it)
                        for n in range(dve_tiles * HEADS, U * HEADS):
                            last = nc.scalar.activation(msg[:, p, n, 0:g.out], rows[:, r, n, 0:g.out], ACT.Copy,
                                                        scale=msg[:, p, n, g.out:])
                            if n == U * HEADS - 1:
                                last.then_inc(s_msga, 1)
                    if now:
                        act.wait_ge(s_drop, it + 1)
                        if not static or it >= RING:
                            act.wait_ge(s_acc, it - (RING - 1))
                        nc.scalar.activation(scale[:, q, :], drop[:, q, :], ACT.Exp).then_inc(s_scale, 1)

                for it in range(2):
                    make_onehot(0, it, it)
                copy_transposed(0, 0)
                by_groups(act, step)
                step(None, G, 0, False, now=False)

            @block.tensor
            def _(pe):
                def step(turn, it, q, near, now=True):
                    static = isinstance(it, int)
                    prev, prev2 = not static or 1 <= it <= G, not static or it >= 2
                    if now or prev:
                        pe.wait_ge(s_oth, it + 1)
                        if not static or it >= 1:
                            pe.wait_ge(s_ot, it)
                        for j in range(U):
                            last = nc.tensor.transpose(ps_ot[:, j, :], onehot[:, q, j, :], ident[:])
                        last.then_inc(s_otp, 1)
                    if now:
                        pe.wait_ge(s_rows[q], (turn + 1) * (16 * U))
                        for j in range(U):
                            if not static or it >= 1:
                                pe.wait_ge(s_mx, it * U + (j + 1 - U))
                            for h in range(HEADS):
                                nc.tensor.matmul(ps_es[:, j, h, :], rows[:, q, j * HEADS + h, g.out:].to_broadcast([P, P]),
                                                 ident[:], start=(h == 0), stop=False, is_transpose=True)
                            nc.tensor.matmul(ps_es[:, j], other[:, q % 2, j, :],
                                             ident_neg[:].unsqueeze(1).to_broadcast([P, HEADS, P]),
                                             start=False, stop=True).then_inc(s_es, 1)
                    if prev:
                        p = (q - 1) % 2
                        pe.wait_ge(s_ot, it)
                        pe.wait_ge(s_node, it)
                        if not static or it >= 2:
                            pe.wait_ge(s_u, it - 1)
                        for j in range(U):
                            last = nc.tensor.matmul(ps_ge[:, p, j, :], onehot_t[:, p, j, :], node[:, p, :], start=True, stop=True)
                        last.then_inc(s_ge, 1)
                    if prev2:
                        p, r = q % 2, (q - 2) % RING
                        pe.wait_ge(s_ex, it - 1)
                        pe.wait_ge(s_msg, it - 1)
                        if dve_tiles < U:
                            pe.wait_ge(s_msga, it - 1)
                        if not static or it >= 4:
                            pe.wait_ge(s_acc, it - 3)
                        for j in range(U):
                            last = nc.tensor.matmul(ps_out[:, p, 0:g.row], onehot[:, r, j, :],
                                                    msg[:, p, j * HEADS:(j + 1) * HEADS, :].rearrange("p h o -> p (h o)"),
                                                    start=(j == 0), stop=(j == U - 1))
                        last.then_inc(s_out, 1)

                by_groups(pe, step)
                for k in range(2):
                    step(None, G + k, k, False, now=False)


def nodes_b(nc, sem, A, B, X, ident, W_gat, att_src, att_dst):
    ph = ExitStack()
    with ph:
        def tb(name, shape, dt=F32):
            return ph.enter_context(nc.sbuf_tensor("nb_" + name, shape, dt))

        K = HEADS * OUT_B
        wx = tb("wx", [P, 2, B.row + HEADS])
        a_bc = tb("a_bc", [P, 2, K])
        wprod = tb("wprod", [P, 2, 2, K])
        rden = tb("rden", [P, BLOCKS, HEADS])
        stats = tb("stats", [P, BLOCKS, 6])
        mean = tb("mean", [P, 3, BLOCKS])
        sd = tb("sd", [P, 2, BLOCKS])
        xn = tb("xn", [P, 2, D])
        xt = tb("xt", [P, 2, 2, P])
        rowsB = tb("rows", [P, BLOCKS, B.row])
        selfs = tb("self", [P, BLOCKS, HEADS])
        ps_t = ph.enter_context(nc.psum_tensor("nb_ps_t", [P, 2, 4, P], F32))
        ps_z = ph.enter_context(nc.psum_tensor("nb_ps_z", [P, 2, 512], F32))
        s_w = sem("nb_w_loaded")
        s_dve = sem("nb_dve_chain")
        s_var, s_sd, s_xn = sem("nb_var"), sem("nb_sd"), sem("nb_xn")
        s_xtp, s_xt, s_z, s_zc = sem("nb_xt_psum"), sem("nb_xt"), sem("nb_z"), sem("nb_z_copied")
        s_tab = sem("nb_table_stored")
        with nc.Block() as block:
            @block.sync
            def _(sp):
                for k in range(2):
                    sp.dma_start(wx[:, k, 0:B.row].rearrange("p (h o) -> p h o", h=HEADS)[:, :, 0:OUT_B],
                                 W_gat[k * P:(k + 1) * P, :].rearrange("p (h o) -> p h o", h=HEADS)).then_inc(s_w, 16)
                for n, a in enumerate((att_src, att_dst)):
                    sp.dma_start(a_bc[:, n, :], a.rearrange("(u h) o -> u (h o)", u=1).to_broadcast([P, K])).then_inc(s_w, 16)
                sp.wait_ge(s_zc, BLOCKS)
                sp.dma_start(B.table.rearrange("(b p) f -> p b f", p=P), rowsB[:]).then_inc(s_tab, 16)
                sp.wait_ge(s_tab, 16)

            @block.vector
            def _(dve):
                link = Chain(dve, s_dve)
                V = nc.vector
                sums = A.acc[:, :, :].rearrange("p b (h o) -> p b h o", h=HEADS)
                x1 = X[:].rearrange("p b (h o) -> p b h o", h=HEADS)
                link(V.tensor_scalar(rden[:], sums[:, :, :, OUT_A], 1e-30, None, ALU.max))
                link(V.reciprocal(rden[:], rden[:]))
                for h in range(HEADS):
                    link.mark(V.tensor_tensor(sums[:, :, h, 0:OUT_A], sums[:, :, h, 0:OUT_A],
                                              rden[:, :, h:h + 1].to_broadcast([P, BLOCKS, OUT_A]), ALU.mult))
                for h in range(HEADS):
                    link.wait(HEADS - 1)
                    link.mark(V.tensor_tensor(x1[:, :, h, :], x1[:, :, h, :], sums[:, :, h, 0:OUT_A], ALU.add))
                link.wait()
                with dve.Fori(0, BLOCKS // PIECE) as c:
                    link.loop(c, PIECE)
                    for b in range(PIECE):
                        one = bass.ds(c * PIECE + b, 1)
                        link.mark(V.bn_stats(stats[:, one, :].rearrange("p b f -> p (b f)"),
                                             X[:, one, :].rearrange("p b f -> p (b f)")))
                    link.end(BLOCKS // PIECE)
                link.wait()
                variance(link, V, stats, mean, sd, s_var)
                dve.wait_ge(s_w, 64)
                for k in range(2):
                    w_ho = wx[:, k, 0:B.row].rearrange("p (h o) -> p h o", h=HEADS)
                    for n in range(2):
                        link.mark(V.tensor_tensor(wprod[:, k, n, :].rearrange("p (h o) -> p h o", h=HEADS), w_ho[:, :, 0:OUT_B],
                                                  a_bc[:, n, :].rearrange("p (h o) -> p h o", h=HEADS), ALU.mult))
                link.wait()
                for k in range(2):
                    w_ho = wx[:, k, 0:B.row].rearrange("p (h o) -> p h o", h=HEADS)
                    for n in range(2):
                        score = w_ho[:, :, OUT_B] if n == 0 else wx[:, k, B.row:]
                        link.mark(V.tensor_reduce(score, wprod[:, k, n, :].rearrange("p (h o) -> p h o", h=HEADS), AXX, ALU.add))
                link.wait()
                dve.wait_ge(s_sd, 1)
                link(V.reciprocal(sd[:, 1, :], sd[:, 1, :]))

                def norm(b, v):
                    one = slice(b, b + 1) if isinstance(b, int) else bass.ds(b, 1)
                    if not isinstance(b, int) or b >= 2:
                        dve.wait_ge(s_xtp, b - 1)
                    V.tensor_scalar(xn[:, v, :], X[:, one, :].rearrange("p b f -> p (b f)"),
                                    mean[:, 0, one], sd[:, 1, one],
                                    ALU.subtract, ALU.mult).then_inc(s_xn, 1)

                def step(b, v, more):
                    if more:
                        norm(b + 2, v)
                    one = slice(b, b + 1) if isinstance(b, int) else bass.ds(b, 1)
                    dve.wait_ge(s_xt, b + 1)
                    V.tensor_scalar(A.acc[:, one, 0:D].rearrange("p b f -> p (b f)"),
                                    xt[:, v].rearrange("p k n -> p (k n)"), 1.0, None, ALU.mult)
                    dve.wait_ge(s_z, b + 1)
                    V.tensor_scalar(rowsB[:, one, :].rearrange("p b f -> p (b f)"), ps_z[:, v, 0:B.row], 1.0, None, ALU.mult)
                    V.tensor_scalar(B.ed[:, one, :].rearrange("p b h -> p (b h)"), ps_z[:, v, B.row:B.row + HEADS],
                                    1.0, None, ALU.mult).then_inc(s_zc, 1)

                norm(0, 0)
                norm(1, 1)
                by_pairs(dve, step)
                dve.wait_ge(s_zc, BLOCKS)
                rows4 = rowsB[:].rearrange("p b (h o) -> p b h o", h=HEADS)
                link(V.tensor_copy(B.acc[:, :, :], rowsB[:]))
                V.memset(B.acc[:, :, :].rearrange("p b (h o) -> p b h o", h=HEADS)[:, :, :, OUT_B], 1.0)
                link(V.tensor_tensor(selfs[:], rows4[:, :, :, OUT_B], B.ed[:, :, :], ALU.add))
                V.scalar_tensor_tensor(B.mx[:, :, :], selfs[:], B.slope, selfs[:], ALU.mult, ALU.max)

            @block.scalar
            def _(act):
                act.wait_ge(s_var, 1)
                nc.scalar.activation(sd[:, 1, :], sd[:, 0, :], ACT.Sqrt).then_inc(s_sd, 1)

                def step(b, v, more):
                    act.wait_ge(s_xtp, b + 1)
                    if not isinstance(b, int) or b >= 2:
                        act.wait_ge(s_zc, b - 1)
                    nc.scalar.activation(xt[:, v], ps_t[:, v, 0:2], ACT.Copy).then_inc(s_xt, 1)

                by_pairs(act, step)

            @block.tensor
            def _(pe):
                def turn_rows(b, v):
                    pe.wait_ge(s_xn, b + 1)
                    if not isinstance(b, int) or b >= 2:
                        pe.wait_ge(s_xt, b - 1)
                    for k in range(2):
                        last = nc.tensor.transpose(ps_t[:, v, k, :], xn[:, v, k * P:(k + 1) * P], ident[:])
                    last.then_inc(s_xtp, 1)

                def step(b, v, more):
                    pe.wait_ge(s_xt, b + 1)
                    if not isinstance(b, int) or b >= 2:
                        pe.wait_ge(s_zc, b - 1)
                    for k in range(2):
                        last = nc.tensor.matmul(ps_z[:, v, 0:B.row + HEADS], xt[:, v, k, :], wx[:, k, :], start=(k == 0), stop=(k == 1))
                    last.then_inc(s_z, 1)
                    if more:
                        turn_rows(b + 2, v)

                turn_rows(0, 0)
                turn_rows(1, 1)
                by_pairs(pe, step)


def experts(nc, sem, A, B, X, w1, w2, b1c, b2b, vec, s_w, all_loaded, out):
    ph = ExitStack()
    with ph:
        def tb(name, shape, dt=F32):
            return ph.enter_context(nc.sbuf_tensor("ex_" + name, shape, dt))

        K = HEADS * OUT_B
        FC = HID // P
        w_ = [tb(f"wk{i}", [P, BLOCKS, K]) for i in range(2)]
        c_ = [tb(f"ck{i}", [P, BLOCKS]) for i in range(6)]
        rden = tb("rden", [P, BLOCKS, HEADS])
        sc = tb("sc", [P, EXPERTS, BLOCKS])
        rank = tb("rank", [P, EXPERTS, BLOCKS])
        terms = tb("terms", [P, EXPERTS, BLOCKS, EXPERTS])
        gate = tb("gate", [P, BLOCKS, EXPERTS])
        hid = tb("hid", [P, 2, FC, P])
        y = tb("y", [P, 2, D])
        ps_h = ph.enter_context(nc.psum_tensor("ex_ps_h", [P, 2, FC, P], F32))
        ps_y = ph.enter_context(nc.psum_tensor("ex_ps_y", [P, 2, 512], F32))
        s_dve, s_va, s_sa, s_sub, s_exp = sem("ex_dve_chain"), sem("ex_var"), sem("ex_std"), sem("ex_sub"), sem("ex_exp")
        s_hp, s_h, s_y, s_add, s_o = sem("ex_hidden_psum"), sem("ex_hidden"), sem("ex_y"), sem("ex_added"), sem("ex_stored")
        with nc.Block() as block:
            @block.sync
            def _(sp):
                for c in range(0, BLOCKS, PIECE):
                    to = min(c + PIECE, BLOCKS - 1)
                    sp.wait_ge(s_add, to * EXPERTS)
                    sp.dma_start(out[c * P:to * P, :].rearrange("(b p) f -> p b f", p=P), X[:, c:to, :]).then_inc(s_o, 16)
                sp.wait_ge(s_add, BLOCKS * EXPERTS)
                sp.dma_start(out[(BLOCKS - 1) * P:N_NODES, :], X[0:TAIL, BLOCKS - 1, :]).then_inc(s_o, 16)
                sp.wait_ge(s_o, 16 * (BLOCKS // PIECE + 1))

            @block.vector
            def _(dve):
                link = Chain(dve, s_dve)
                V = nc.vector
                dve.wait_ge(s_w, all_loaded)
                acc4 = B.acc[:, :, :].rearrange("p b (h o) -> p b h o", h=HEADS)
                link(V.tensor_scalar(rden[:], acc4[:, :, :, OUT_B], 1e-16, None, ALU.add))
                link(V.reciprocal(rden[:], rden[:]))
                agg = w_[0][:]
                for h in range(HEADS):
                    link.mark(V.tensor_tensor(agg[:, :, h * OUT_B:(h + 1) * OUT_B], acc4[:, :, h, 0:OUT_B],
                                              rden[:, :, h:h + 1].to_broadcast([P, BLOCKS, OUT_B]), ALU.mult))
                link.wait()

                def bc(n):
                    return vec[:, n, :].unsqueeze(1).to_broadcast([P, BLOCKS, K])

                def col(c):
                    return c.unsqueeze(2).to_broadcast([P, BLOCKS, K])

                link(V.tensor_tensor(agg, agg, bc(0), ALU.add))
                mean, var, inv = c_[0][:], c_[1][:], c_[2][:]
                link(V.tensor_reduce(mean, agg, AXX, ALU.add))
                link(V.tensor_scalar(mean, mean, 1.0 / K, None, ALU.mult))
                link(V.tensor_tensor(agg, agg, col(mean), ALU.subtract))
                link(V.tensor_tensor(w_[1][:], agg, agg, ALU.mult))
                link(V.tensor_reduce(var, w_[1][:], AXX, ALU.add))
                V.tensor_scalar(var, var, 1.0 / K, LN_EPS, ALU.mult, ALU.add).then_inc(s_va, 1)
                dve.wait_ge(s_sa, 1)
                link(V.reciprocal(inv, inv))
                link(V.tensor_tensor(agg, agg, col(inv), ALU.mult))
                link(V.tensor_tensor(agg, agg, bc(1), ALU.mult))
                link(V.tensor_tensor(agg, agg, bc(2), ALU.add))
                for e in range(EXPERTS):
                    link.mark(V.tensor_reduce(sc[:, e, :], agg.rearrange("p b (h o) -> p b h o", h=HEADS)[:, :, :, e], AXX, ALU.add))
                link.wait()
                link(V.tensor_scalar(sc[:], sc[:], 1.0 / HEADS, None, ALU.mult))
                for e in range(EXPERTS):
                    for k, o in enumerate(o for o in range(EXPERTS) if o != e):
                        link.mark(V.tensor_tensor(terms[:, e, :, k], sc[:, o, :], sc[:, e, :], ALU.is_ge if o < e else ALU.is_gt))
                link.wait()
                link(V.tensor_reduce(rank[:], terms[:, :, :, 0:EXPERTS - 1], AXX, ALU.add))
                first, second = c_[4][:], c_[5][:]
                for n in range(2):
                    for e in range(EXPERTS):
                        link.mark(V.scalar_tensor_tensor(terms[:, n, :, e], rank[:, e, :], float(n), sc[:, e, :], ALU.is_equal, ALU.mult))
                link.wait()
                link.mark(V.tensor_reduce(first, terms[:, 0], AXX, ALU.add))
                link(V.tensor_reduce(second, terms[:, 1], AXX, ALU.add))
                V.tensor_tensor(second, second, first, ALU.subtract).then_inc(s_sub, 1)
                dve.wait_ge(s_exp, 1)
                link(V.tensor_scalar(first, second, 1.0, None, ALU.add))
                link(V.reciprocal(first, first))
                link(V.tensor_tensor(second, second, first, ALU.mult))
                for e in range(EXPERTS):
                    link.mark(V.scalar_tensor_tensor(terms[:, 0, :, e], rank[:, e, :], 0.0, first, ALU.is_equal, ALU.mult))
                    link.mark(V.scalar_tensor_tensor(terms[:, 1, :, e], rank[:, e, :], 1.0, second, ALU.is_equal, ALU.mult))
                link.wait()
                link(V.tensor_tensor(gate[:], terms[:, 0], terms[:, 1], ALU.add))
                with dve.Fori(0, BLOCKS) as b:
                    link.loop(b, EXPERTS)
                    xb = X[:, bass.ds(b, 1), :].rearrange("p b f -> p (b f)")
                    for e in range(EXPERTS):
                        dve.wait_ge(s_y, b * EXPERTS + (e + 1))
                        link(V.tensor_tensor(y[:, e % 2, :], ps_y[:, e % 2, 0:D], b2b[:, e, :], ALU.add))
                        V.scalar_tensor_tensor(xb, y[:, e % 2, :], gate[:, bass.ds(b, 1), e:e + 1].rearrange("p b e -> p (b e)"),
                                               xb, ALU.mult, ALU.add).then_inc(s_add, 1)
                    link.end(BLOCKS)

            @block.scalar
            def _(act):
                act.wait_ge(s_va, 1)
                nc.scalar.activation(c_[2][:], c_[1][:], ACT.Sqrt).then_inc(s_sa, 1)
                act.wait_ge(s_sub, 1)
                nc.scalar.activation(c_[5][:], c_[5][:], ACT.Exp).then_inc(s_exp, 1)
                act.wait_ge(s_w, all_loaded)

                def gelu(b, e):
                    act.wait_ge(s_hp, b * EXPERTS + (e + 1))
                    if not isinstance(b, int) or b or e >= 2:
                        act.wait_ge(s_y, b * EXPERTS + (e - 1))
                    for c in range(FC):
                        last = nc.scalar.activation(hid[:, e % 2, c, :], ps_h[:, e % 2, c, :], ACT.Gelu, bias=b1c[:, e, c:c + 1])
                    last.then_inc(s_h, 1)

                for e in range(EXPERTS):
                    gelu(0, e)
                with act.Fori(1, BLOCKS) as b:
                    for e in range(EXPERTS):
                        gelu(b, e)

            @block.tensor
            def _(pe):
                pe.wait_ge(s_w, all_loaded)

                def up(b, e):
                    if not isinstance(b, int) or b or e >= 2:
                        pe.wait_ge(s_h, b * EXPERTS + (e - 1))
                    bs = bass.ds(b, 1) if not isinstance(b, int) else slice(b, b + 1)
                    for c in range(FC):
                        for k in range(2):
                            last = nc.tensor.matmul(ps_h[:, e % 2, c, :], w1[:, e, k, c * P:(c + 1) * P],
                                                    A.acc[:, bs, k * P:(k + 1) * P].rearrange("p b n -> p (b n)"),
                                                    start=(k == 0), stop=(k == 1))
                    last.then_inc(s_hp, 1)

                def down(b, e):
                    pe.wait_ge(s_h, b * EXPERTS + (e + 1))
                    if not isinstance(b, int) or b or e >= 2:
                        pe.wait_ge(s_add, b * EXPERTS + (e - 1))
                    for c in range(FC):
                        last = nc.tensor.matmul(ps_y[:, e % 2, 0:D], hid[:, e % 2, c, :], w2[:, e, c, :], start=(c == 0), stop=(c == FC - 1))
                    last.then_inc(s_y, 1)

                def node_block(b, more):
                    for e in range(EXPERTS):
                        if e + 1 < EXPERTS:
                            up(b, e + 1)
                        elif more:
                            up(b + 1, 0)
                        down(b, e)

                up(0, 0)
                node_block(0, True)
                with pe.Fori(1, BLOCKS - 1) as b:
                    node_block(b, True)
                node_block(BLOCKS - 1, False)


_INS = ['x', 'src', 'dst', 'L0_gnn_W', 'L0_gnn_a_src', 'L0_gnn_a_dst', 'L0_ffn_W_gat', 'L0_ffn_att_src',
        'L0_ffn_att_dst', 'L0_ffn_b_gat', 'L0_ffn_ln_gamma', 'L0_ffn_ln_beta', 'L0_ffn_W1', 'L0_ffn_b1',
        'L0_ffn_W2', 'L0_ffn_b2', 'L0_ffn_edge_index']


def kernel(**inputs):
    import numpy as _np
    import concourse.bacc as _bacc
    from concourse import mybir as _mybir
    from concourse.bass_utils import run_bass_kernel_spmd as _run

    nc = _bacc.Bacc("TRN2", target_bir_lowering=False, num_devices=1)
    arrays, args = {}, []
    for name in _INS:
        a = _np.ascontiguousarray(inputs[name])
        arrays[f"in_{name}"] = a
        args.append(nc.dram_tensor(f"in_{name}", a.shape, _mybir.dt.from_np(a.dtype), kind="ExternalInput").ap())
    args.append(nc.dram_tensor("out_0", (N_NODES, D), F32, kind="ExternalOutput").ap())
    build(nc, *args)
    r = _run(nc, [arrays], core_ids=[0])
    return r.results[0]["out_0"]
```
